# Optimizing a Trainium2 kernel written in Bass

```python
import numpy as np
import jax
import jax.numpy as jnp

def _softmax(x, axis=-1):
    return jax.nn.softmax(x, axis=axis)

def _gelu(x):
    return jax.nn.gelu(x, approximate=True)

def _silu(x):
    return jax.nn.silu(x)

def _sigmoid(x):
    return jax.nn.sigmoid(x)

def _layernorm(x, axis=-1, eps=1e-05):
    m = jnp.mean(x, axis=axis, keepdims=True)
    v = jnp.var(x, axis=axis, keepdims=True)
    return (x - m) / jnp.sqrt(v + eps)

def _scatter_add(tgt, idx, src, axis=0):
    return tgt.at[idx].add(src)

def _segment_sum(src, seg, n):
    return jax.ops.segment_sum(src, seg, n)
kernel_name = 'mk_seq_postln_d1_jaxref_r8_7f67aa'

def setup_inputs(seed: int=0):
    np.random.seed(seed)
    _w = jnp.asarray

    def _L0_attn_setup():
        import jax, jax.numpy as jnp
        import numpy as np
        ROPE_THETA = 10000.0

        def rope(t, rot_dim):
            S = t.shape[-2]
            half = rot_dim // 2
            inv_freq = 1.0 / ROPE_THETA ** (jnp.arange(0, rot_dim, 2, dtype=jnp.float32) / rot_dim)
            freqs = jnp.arange(S, dtype=jnp.float32)[:, None] * inv_freq[None, :]
            freqs = jnp.repeat(freqs, 2, axis=-1)
            cos, sin = (jnp.cos(freqs), jnp.sin(freqs))
            t_rot, t_pass = (t[..., :rot_dim], t[..., rot_dim:])
            x = t_rot.reshape(*t_rot.shape[:-1], half, 2)
            rh = jnp.stack([-x[..., 1], x[..., 0]], axis=-1).reshape(t_rot.shape)
            t_rot = t_rot * cos + rh * sin
            return jnp.concatenate([t_rot, t_pass], axis=-1)

        def feature_map(x):
            norm = jnp.sqrt(jnp.sum(x * x, axis=-1, keepdims=True))
            return x / jnp.maximum(norm, 1e-12)
        key = jax.random.key(seed)
        kx, kwi, kwo = jax.random.split(key, 3)
        B, S, D = (8, 512, 256)
        scale = 0.02
        return {'X': jax.random.normal(kx, (B, S, D), dtype=jnp.float32), 'W_in': jax.random.normal(kwi, (3 * D, D), dtype=jnp.float32) * scale, 'b_in': jnp.zeros((3 * D,), dtype=jnp.float32), 'W_out': jax.random.normal(kwo, (D, D), dtype=jnp.float32) * scale, 'b_out': jnp.zeros((D,), dtype=jnp.float32)}
    _L0_attn_in = _L0_attn_setup()

    def _L0_ffn_setup():
        import jax, jax.numpy as jnp
        import numpy as np
        NUM_EXPERTS = 8
        HIDDEN = 256
        INTER = 256
        TOP_K = 2
        key = jax.random.key(seed)
        ks = jax.random.split(key, 7)
        hidden_states = jax.random.normal(ks[0], (4, 256, HIDDEN), dtype=jnp.float32)
        gate_w = jax.random.normal(ks[1], (HIDDEN, NUM_EXPERTS), dtype=jnp.float32) * 0.02
        fc1_w = jax.random.normal(ks[2], (NUM_EXPERTS, HIDDEN, INTER), dtype=jnp.float32) * 0.02
        fc1_b = jnp.zeros((NUM_EXPERTS, INTER), dtype=jnp.float32)
        fc2_w = jax.random.normal(ks[3], (NUM_EXPERTS, INTER, HIDDEN), dtype=jnp.float32) * 0.02
        fc2_b = jnp.zeros((NUM_EXPERTS, HIDDEN), dtype=jnp.float32)
        alpha = jax.random.normal(ks[4], (NUM_EXPERTS,), dtype=jnp.float32)
        return {'hidden_states': hidden_states, 'gate_w': gate_w, 'fc1_w': fc1_w, 'fc1_b': fc1_b, 'fc2_w': fc2_w, 'fc2_b': fc2_b, 'alpha': alpha}
    _L0_ffn_in = _L0_ffn_setup()
    _d = {'L0_attn_X': _L0_attn_in['X'], 'L0_attn_W_in': _L0_attn_in['W_in'], 'L0_attn_b_in': _L0_attn_in['b_in'], 'L0_attn_W_out': _L0_attn_in['W_out'], 'L0_attn_b_out': _L0_attn_in['b_out'], 'L0_ffn_gate_w': _L0_ffn_in['gate_w'], 'L0_ffn_fc1_w': _L0_ffn_in['fc1_w'], 'L0_ffn_fc1_b': _L0_ffn_in['fc1_b'], 'L0_ffn_fc2_w': _L0_ffn_in['fc2_w'], 'L0_ffn_fc2_b': _L0_ffn_in['fc2_b'], 'L0_ffn_alpha': _L0_ffn_in['alpha']}
    _x0 = _d['L0_attn_X']
    _d['L0_attn_X'] = jax.random.normal(jax.random.fold_in(jax.random.key(seed), 1), (1, 1024, 256), dtype=_x0.dtype)
    del _x0
    return _d

def reference(L0_attn_X, L0_attn_W_in, L0_attn_b_in, L0_attn_W_out, L0_attn_b_out, L0_ffn_gate_w, L0_ffn_fc1_w, L0_ffn_fc1_b, L0_ffn_fc2_w, L0_ffn_fc2_b, L0_ffn_alpha):

    def _L0_attn_ref(X, W_in, b_in, W_out, b_out):
        import jax, jax.numpy as jnp
        import numpy as np
        ROPE_THETA = 10000.0

        def rope(t, rot_dim):
            S = t.shape[-2]
            half = rot_dim // 2
            inv_freq = 1.0 / ROPE_THETA ** (jnp.arange(0, rot_dim, 2, dtype=jnp.float32) / rot_dim)
            freqs = jnp.arange(S, dtype=jnp.float32)[:, None] * inv_freq[None, :]
            freqs = jnp.repeat(freqs, 2, axis=-1)
            cos, sin = (jnp.cos(freqs), jnp.sin(freqs))
            t_rot, t_pass = (t[..., :rot_dim], t[..., rot_dim:])
            x = t_rot.reshape(*t_rot.shape[:-1], half, 2)
            rh = jnp.stack([-x[..., 1], x[..., 0]], axis=-1).reshape(t_rot.shape)
            t_rot = t_rot * cos + rh * sin
            return jnp.concatenate([t_rot, t_pass], axis=-1)

        def feature_map(x):
            norm = jnp.sqrt(jnp.sum(x * x, axis=-1, keepdims=True))
            return x / jnp.maximum(norm, 1e-12)
        D = X.shape[-1]
        QKV = jnp.einsum('bsd,ed->bse', X, W_in) + b_in
        Q, K, V = jnp.split(QKV, 3, axis=-1)
        rot_dim = D // 2
        Q = rope(Q, rot_dim)
        K = rope(K, rot_dim)
        A = jnp.sum(feature_map(K) * V, axis=-2)
        Y = A[:, None, :] * Q
        Y = jnp.einsum('bsd,ed->bse', Y, W_out) + b_out
        return Y + X

    def _L0_ffn_ref(hidden_states, gate_w, fc1_w, fc1_b, fc2_w, fc2_b, alpha):
        import jax, jax.numpy as jnp
        import numpy as np
        NUM_EXPERTS = 8
        HIDDEN = 256
        INTER = 256
        TOP_K = 2
        B, S, H = hidden_states.shape
        x = hidden_states.reshape(-1, H)
        probs = jax.nn.softmax(x @ gate_w, axis=-1)
        gate_score, gate_idx = jax.lax.top_k(probs, TOP_K)
        gate_score = gate_score / jnp.sum(gate_score, axis=-1, keepdims=True)
        onehot = jax.nn.one_hot(gate_idx, NUM_EXPERTS, dtype=x.dtype)
        combine = jnp.einsum('tk,tke->te', gate_score, onehot) * alpha[None, :]
        h = jnp.einsum('th,ehi->eti', x, fc1_w) + fc1_b[:, None, :]
        h = jax.nn.gelu(h, approximate=False)
        y = jnp.einsum('eti,eih->eth', h, fc2_w) + fc2_b[:, None, :]
        out = jnp.einsum('eth,te->th', y, combine)
        return out.reshape(B, S, H)
    x = L0_attn_X
    x = _layernorm(x + _L0_attn_ref(x, L0_attn_W_in, L0_attn_b_in, L0_attn_W_out, L0_attn_b_out), axis=-1)
    x = _layernorm(x + _L0_ffn_ref(x, L0_ffn_gate_w, L0_ffn_fc1_w, L0_ffn_fc1_b, L0_ffn_fc2_w, L0_ffn_fc2_b, L0_ffn_alpha), axis=-1)
    return x

_drawn_inputs = setup_inputs


def setup_inputs(seed=0):
    import zlib

    import numpy as np

    out = dict(_drawn_inputs(seed))
    spreads = {'L0_attn_b_in': (0.0, 0.1),
     'L0_attn_b_out': (0.0, 0.1),
     'L0_ffn_fc1_b': (0.0, 0.59),
     'L0_ffn_fc2_b': (0.0, 0.1)}
    factors = {}
    for name, (base, spread) in spreads.items():
        noise = np.random.default_rng([zlib.crc32(name.encode()), seed]).standard_normal(out[name].shape)
        drawn = base * np.exp(spread * noise) if base else spread * noise
        out[name] = jnp.asarray(drawn.astype(out[name].dtype))
    for name, factor in factors.items():
        out[name] = (out[name] * factor).astype(out[name].dtype)
    return out
```

```python
from contextlib import ExitStack

import numpy as np

import concourse.bass as bass
from concourse import mybir

ALU = mybir.AluOpType
ACT = mybir.ActivationFunctionType
AX_X = mybir.AxisListType.X
F32 = mybir.dt.float32
F32R = mybir.dt.float32r

P = 128
ROPE_THETA = 10000.0
LN_EPS = 1e-5
NORM_FLOOR = 1e-12
MASKED = -3.0e38


def layer_kernel(nc, x_tok, x_t, w_kv_t, w_q_t, w_out_t, b_kv, b_q, b_out, rope_tok, rope_t,
                 gate_w, expert_w, fc1_b, fc2_b, alpha, tie_order, out):
    _, T, D = x_tok.shape
    S = T * P
    KD = D // P
    E = expert_w.shape[0]
    ROT = 2 * rope_tok.shape[-1]
    HALF = rope_tok.shape[-1]
    NH = S // 512
    TPH = T // NH
    assert (D, KD, NH, E, T) == (256, 2, 2, 8, 8)

    with ExitStack() as ctx:
        def sb(name, shape, dt=F32):
            return ctx.enter_context(nc.sbuf_tensor(name, shape, dt))

        def sem(name):
            return ctx.enter_context(nc.semaphore(name))

        ps = ctx.enter_context(nc.psum_tensor("ps", [P, 8, 512], F32))

        xT = sb("xT", [P, KD, S])
        wkv = sb("wkv", [P, KD, 2 * D])
        wq = sb("wq", [P, KD, D + ROT])
        wout = sb("wout", [P, KD, D])
        bkv = sb("bkv", [P, 2 * D])
        bq = sb("bq", [P, 3])
        bout = sb("bout", [P, D])
        rtok = sb("rtok", [P, 2, T, HALF])
        rT = sb("rT", [P, 2, S])
        gw = sb("gw", [P, KD, E])
        wraw = sb("wraw", [P, 2, 4 * D])
        b1 = sb("b1", [P, E, KD])
        b1_now = sb("b1_now", [P, 2, KD])
        b2 = sb("b2", [2 * E, D])
        alp = sb("alp", [P, E])
        order = sb("order", [P, E])

        fT_hi = sb("fT_hi", [P, KD, S], F32R)
        fT_lo = sb("fT_lo", [P, KD, S], F32R)
        wkv_hi = sb("wkv_hi", [P, KD, 2 * D], F32R)
        wkv_lo = sb("wkv_lo", [P, KD, 2 * D], F32R)
        wq_hi = sb("wq_hi", [P, KD, D + ROT], F32R)
        wq_lo = sb("wq_lo", [P, KD, D + ROT], F32R)
        kv = sb("kv", [P, T, 2 * D])
        ksq = sb("ksq", [P, T])
        knorm = sb("knorm", [P, T])
        kfloor = sb("kfloor", [P, T])
        krec = sb("krec", [P, T])
        acol = sb("acol", [P, KD])
        wo_hi = sb("wo_hi", [P, KD, D], F32R)
        wo_lo = sb("wo_lo", [P, KD, D], F32R)
        qa = sb("qa", [P, NH, 512])
        qb = sb("qb", [P, NH, 512])
        qT = sb("qT", [P, KD, S])
        gT_hi = sb("gT_hi", [P, KD, S], F32R)
        gT_lo = sb("gT_lo", [P, KD, S], F32R)

        z = sb("z", [P, T, D])
        acc = sb("acc", [P, T, D])
        x1 = sb("x1", [P, T, D])
        rot_a, rot_b = (x1[:, i * T // 2:(i + 1) * T // 2, :].rearrange("p t (u r) -> p (t u) r", r=ROT)
                        for i in range(2))
        stats = sb("stats", [P, T, 6])
        mv = sb("mv", [P, T, 2])
        sd = sb("sd", [P, T])
        rstd = sb("rstd", [P, T])
        ident = sb("ident", [P, P])
        eps = sb("eps", [P, 1])
        zero = sb("zero", [P, 1])

        gpad = sb("gpad", [P, KD, P], F32R)
        lgT = sb("lgT", [2 * E, S])
        lgp = sb("lgp", [P, T, 2 * E])
        lg = sb("lg", [P, T, E])
        lg2 = sb("lg2", [P, T, E])
        hit = sb("hit", [P, T, E])
        sel = sb("sel", [P, 2, T, E])
        top = sb("top", [P, 2, T])
        which = sb("which", [P, 2, T])
        gap = sb("gap", [P, T])
        th = sb("th", [P, T])
        wt = sb("wt", [P, 2, T])
        comb = sb("comb", [P, T, E])
        comb_p = sb("comb_p", [P, T, 2 * E])
        combT = sb("combT", [2 * E, S], F32R)
        b2_hi = sb("b2_hi", [2 * E, D], F32R)
        b2_lo = sb("b2_lo", [2 * E, D], F32R)

        w_hi = sb("w_hi", [P, 2, 4 * D], F32R)
        w_lo = sb("w_lo", [P, 2, 4 * D], F32R)
        h = kv[:, 0:2 * NH, :]

        l_wkv, l_wq, l_wout, l_bkv, l_bq, l_bout, l_rtok, l_rT, l_small, l_x = (
            sem(f"l_{n}") for n in "wkv wq wout bkv bq bout rtok rT small x".split())
        l_xT = [sem(f"l_xT{c}") for c in range(4)]
        l_exp = [sem(f"l_exp{slot}") for slot in range(2)]
        stored = sem("stored")
        wkv_hi_ok, wkv_lo_ok, xT_hi_ok, xT_lo_ok, wq_hi_ok, wq_lo_ok = (
            sem(n) for n in "wkv_hi_ok wkv_lo_ok xT_hi_ok xT_lo_ok wq_hi_ok wq_lo_ok".split())
        kv_mm, kv_ok, rot_parts, rot_ok, kv_prod, ksq_ok, knorm_ok, kfloor_ok, krec_ok = (
            sem(n) for n in "kv_mm kv_ok rot_parts rot_ok kv_prod ksq_ok knorm_ok kfloor_ok krec_ok".split())
        q_mm, qab_ok, q_rot_ok, q_pass_ok, q_hi_ok, q_lo_ok = (
            sem(n) for n in "q_mm qab_ok q_rot_ok q_pass_ok q_hi_ok q_lo_ok".split())
        a_mm, acol_ok, wo_hi_ok, wo_lo_ok = (sem(n) for n in "a_mm acol_ok wo_hi_ok wo_lo_ok".split())
        o_mm, res_dbl, res_ok, z_ok, stats_ok, mv_ok, sd_ok, rstd_ok, x1_ok, x1T_mm, x1_hi_ok, x1_lo_ok = (
            sem(n) for n in "o_mm res_dbl res_ok z_ok stats_ok mv_ok sd_ok rstd_ok x1_ok x1T_mm x1_hi_ok x1_lo_ok".split())
        ident0, ident_ok, gpad0, gate_hi_ok, gate_ok, b2_hi_ok, b2_ok = (
            sem(n) for n in "ident0 ident_ok gpad0 gate_hi_ok gate_ok b2_hi_ok b2_ok".split())
        lg_mm, lgT_ok, lgp_mm, lgp_ok, route, gap_ok, th_ok, comb_p_ok, combT_mm, combT_ok, bias_mm, bias_ok = (
            sem(n) for n in "lg_mm lgT_ok lgp_mm lgp_ok route gap_ok th_ok comb_p_ok combT_mm combT_ok bias_mm bias_ok".split())
        const_ok, b1_ok, w_part, w1_ok, w2_ok, fc1_mm, h_ok, g_hi_ok, g_lo_ok, y_mm, y_ok = (
            sem(n) for n in "const_ok b1_ok w_part w1_ok w2_ok fc1_mm h_ok g_hi_ok g_lo_ok y_mm y_ok".split())
        stats2_ok, mv2_ok, sd2_ok, rstd2_ok, out_ok = (
            sem(n) for n in "stats2_ok mv2_ok sd2_ok rstd2_ok out_ok".split())

        def raw(part):
            return part.bitcast(F32)

        def half(n):
            return slice(n * 512, (n + 1) * 512)

        def tile(t):
            return slice(t * P, (t + 1) * P)

        block = ctx.enter_context(nc.Block())

        @block.sync
        def _(sp):
            sp.dma_start(wkv[:], w_kv_t).then_inc(l_wkv, 16)
            for c in range(4):
                cols = slice(c * 256, (c + 1) * 256)
                sp.dma_start(xT[:, :, cols], x_t[:, :, cols]).then_inc(l_xT[c], 16)
            sp.dma_start(rtok[:], rope_tok).then_inc(l_rtok, 16)
            sp.dma_start(wq[:], w_q_t).then_inc(l_wq, 16)
            sp.dma_start(rT[:], rope_t).then_inc(l_rT, 16)
            sp.dma_start(wout[:], w_out_t).then_inc(l_wout, 16)
            sp.dma_start(acc[:], x_tok).then_inc(l_x, 16)
            for e in range(2):
                sp.dma_start(wraw[:, e, :], expert_w[e]).then_inc(l_exp[e], 16)
            with sp.Fori(1, E // 2) as pair:
                for slot in range(2):
                    sp.wait_ge(w2_ok, pair * 2 + (slot - 1))
                    sp.dma_start(wraw[:, slot, :], expert_w[bass.ds(pair * 2 + slot, 1)].squeeze(0))\
                      .then_inc(l_exp[slot], 16)
            for j in range(T // 2):
                sp.wait_ge(out_ok, 2 * j + 2)
                sp.dma_start(out[2 * j * P:(2 * j + 2) * P, :].rearrange("(t p) d -> p t d", p=P),
                             z[:, 2 * j:2 * j + 2, :]).then_inc(stored, 16)
            sp.wait_ge(stored, 16 * (T // 2))

        @block.gpsimd
        def _(pool):
            g = nc.gpsimd
            g.memset(ident[:], 0.0).then_inc(ident0, 1)
            g.memset(zero[:], 0.0).then_inc(const_ok, 1)
            g.memset(eps[:], LN_EPS).then_inc(const_ok, 1)
            g.memset(raw(gpad[:]), 0.0).then_inc(gpad0, 1)
            pool.wait_ge(ident0, 1)
            g.affine_select(out=ident[:], in_=ident[:], compare_op=ALU.not_equal, fill=1.0, base=0,
                            pattern=[[-1, P]], channel_multiplier=1).then_inc(ident_ok, 1)
            pool.wait_ge(l_rtok, 16)
            for j in range(T // 2):
                two = slice(2 * j, 2 * j + 2)
                k_pair = kv[:, two, 0:ROT].rearrange("p t (i c) -> p t i c", c=2)
                a_pair = rot_a[:, two, :].rearrange("p t (i c) -> p t i c", c=2)
                b_pair = rot_b[:, two, :].rearrange("p t (i c) -> p t i c", c=2)
                pool.wait_ge(kv_ok, 2 * j + 2)
                for c in range(2):
                    g.tensor_tensor(a_pair[:, :, :, c], k_pair[:, :, :, c], rtok[:, 0, two, :], ALU.mult)
                    g.tensor_tensor(b_pair[:, :, :, c], k_pair[:, :, :, 1 - c], rtok[:, 1, two, :],
                                    ALU.mult).then_inc(rot_parts, 1)
                pool.wait_ge(rot_parts, 2 * j + 2)
                g.tensor_tensor(k_pair[:, :, :, 0], a_pair[:, :, :, 0], b_pair[:, :, :, 0], ALU.subtract)
                g.tensor_tensor(k_pair[:, :, :, 1], a_pair[:, :, :, 1], b_pair[:, :, :, 1],
                                ALU.add).then_inc(rot_ok, 1)
            pool.wait_ge(l_x, 16)
            g.tensor_tensor(acc[:], acc[:], acc[:], ALU.add).then_inc(res_dbl, 1)
            pool.wait_ge(l_bout, 16)
            pool.wait_ge(res_dbl, 1)
            g.tensor_tensor(acc[:], acc[:], bout[:].unsqueeze(1).to_broadcast([P, T, D]),
                            ALU.add).then_inc(res_ok, 1)
            for n in range(NH):
                pool.wait_ge(qab_ok, 2 * n + 2)
                g.tensor_tensor(qT[:, 0, half(n)], qa[:, n, :], qb[:, n, :], ALU.add).then_inc(q_rot_ok, 1)
            pool.wait_ge(l_small, 5 * 16)
            pool.wait_ge(gpad0, 1)
            g.tensor_copy(gpad[:, :, 0:E], gw[:]).then_inc(gate_hi_ok, 1)
            g.tensor_copy(b2_hi[:], b2[:]).then_inc(b2_hi_ok, 1)
            pool.wait_ge(gate_hi_ok, 1)
            g.tensor_tensor(gpad[:, :, E:2 * E], gw[:], raw(gpad[:, :, 0:E]), ALU.subtract).then_inc(gate_ok, 1)
            pool.wait_ge(b2_hi_ok, 1)
            g.tensor_tensor(b2_lo[:], b2[:], raw(b2_hi[:]), ALU.subtract).then_inc(b2_ok, 1)

            def split(slot, part, n_parts, ok):
                cols = slice(part * 2 * D, (part + 1) * 2 * D)
                src = wraw[:, slot, cols]
                g.tensor_tensor(w_hi[:, slot, cols], src, zero[:].to_broadcast([P, 2 * D]),
                                ALU.add).then_inc(w_part, 1)
                pool.wait_ge(w_part, n_parts)
                g.tensor_tensor(w_lo[:, slot, cols], src, raw(w_hi[:, slot, cols]), ALU.subtract).then_inc(ok, 1)

            pool.wait_ge(const_ok, 1)
            for e in range(2):
                pool.wait_ge(l_exp[e], 16)
                split(e, 0, 2 * e + 1, w1_ok)
                split(e, 1, 2 * e + 2, w2_ok)
            with pool.Fori(1, E // 2) as pair:
                e0 = pair * 2
                for slot in range(2):
                    pool.wait_ge(l_exp[slot], pair * 16 + 16)
                    pool.wait_ge(fc1_mm, e0 * 4 + (4 * slot - 4))
                    split(slot, 0, e0 * 2 + (2 * slot + 1), w1_ok)
                    pool.wait_ge(y_mm, e0 * 4 + (4 * slot - 4))
                    split(slot, 1, e0 * 2 + (2 * slot + 2), w2_ok)

        @block.scalar
        def _(act):
            a = nc.scalar
            act.dma_start(bkv[:], b_kv.partition_broadcast(P)).then_inc(l_bkv, 16)
            act.dma_start(bq[:], b_q).then_inc(l_bq, 16)
            act.dma_start(bout[:], b_out.partition_broadcast(P)).then_inc(l_bout, 16)
            act.dma_start(gw[:], gate_w).then_inc(l_small, 16)
            act.dma_start(b1[:], fc1_b).then_inc(l_small, 16)
            act.dma_start(b2[:], fc2_b).then_inc(l_small, 16)
            act.dma_start(alp[:], alpha.partition_broadcast(P)).then_inc(l_small, 16)
            act.dma_start(order[:], tie_order.partition_broadcast(P)).then_inc(l_small, 16)
            act.wait_ge(l_wkv, 16)
            a.copy(wkv_hi[:], wkv[:]).then_inc(wkv_hi_ok, 1)
            for c in range(4):
                cols = slice(c * 256, (c + 1) * 256)
                act.wait_ge(l_xT[c], 16)
                a.copy(fT_hi[:, :, cols], xT[:, :, cols]).then_inc(xT_hi_ok, 1)
            act.wait_ge(l_wq, 16)
            a.copy(wq_hi[:], wq[:]).then_inc(wq_hi_ok, 1)
            for t in range(T):
                act.wait_ge(rot_ok, t // 2 + 1)
                a.activation(gT_lo[:, t // TPH, (t % TPH) * D:(t % TPH + 1) * D], kv[:, t, 0:D], ACT.Square, accum_out=ksq[:, t:t + 1]).then_inc(ksq_ok, 1)
                if t % TPH == TPH - 1:
                    act.wait_ge(ksq_ok, t + 1)
                    q4 = slice(t - TPH + 1, t + 1)
                    a.activation(knorm[:, q4], ksq[:, q4], ACT.Sqrt).then_inc(knorm_ok, 1)
            act.wait_ge(l_bq, 16)
            for n in range(NH):
                act.wait_ge(q_mm, 3 * n + 3)
                a.activation(qT[:, 1, half(n)], ps[:, (6, 1)[n], :], ACT.Identity,
                             bias=bq[:, 1:2]).then_inc(q_pass_ok, 1)
                act.wait_ge(q_pass_ok, n + 1)
                act.wait_ge(q_rot_ok, n + 1)
                a.copy(gT_hi[:, :, half(n)], qT[:, :, half(n)]).then_inc(q_hi_ok, 1)

            def root(j):
                act.wait_ge(mv_ok, 2 * j + 2)
                a.activation(sd[:, 2 * j:2 * j + 2], mv[:, 2 * j:2 * j + 2, 1], ACT.Sqrt,
                             bias=eps[:]).then_inc(sd_ok, 1)

            def x1_high(t):
                act.wait_ge(x1T_mm, t + 1)
                a.copy(fT_hi[:, :, tile(t)], ps[:, 2 + t % 2, 0:D].rearrange("p (k c) -> p k c", k=KD))\
                 .then_inc(x1_hi_ok, 1)

            act.wait_ge(const_ok, 2)
            root(0)
            root(1)
            x1_high(0)
            x1_high(1)
            root(2)
            x1_high(2)
            x1_high(3)
            root(3)
            for t in range(4, T):
                x1_high(t)

            def gelu(e, n, m, bias):
                i = 2 * n + m
                act.wait_ge(fc1_mm, e * 4 + (i + 1))
                if not isinstance(e, int) or e > 0:
                    act.wait_ge(g_lo_ok, e * 4 + (i - 3))
                a.activation(h[:, i, :], ps[:, i, :], ACT.Gelu, bias=bias[:, m:m + 1]).then_inc(h_ok, 1)
                act.wait_ge(h_ok, e * 4 + (i + 1))
                a.copy(gT_hi[:, m, half(n)], h[:, i, :]).then_inc(g_hi_ok, 1)

            act.wait_ge(l_small, 5 * 16)
            gelu(0, 0, 0, b1[:, 0, :])
            for n in range(NH):
                act.wait_ge(lg_mm, n + 1)
                a.copy(lgT[:, half(n)], ps[0:2 * E, 4 + n, :]).then_inc(lgT_ok, 1)
            gelu(0, 0, 1, b1[:, 0, :])
            gelu(0, 1, 0, b1[:, 0, :])
            act.wait_ge(lgp_mm, 1)
            a.copy(lgp[:], ps[:, 6, 0:T * 2 * E].rearrange("p (t c) -> p t c", t=T)).then_inc(lgp_ok, 1)
            gelu(0, 1, 1, b1[:, 0, :])
            act.wait_ge(gap_ok, 1)
            a.activation(th[:], gap[:], ACT.Tanh, scale=0.5).then_inc(th_ok, 1)
            for n in range(NH):
                for m in range(KD):
                    gelu(1, n, m, b1[:, 1, :])
            for c in range(2):
                act.wait_ge(combT_mm, c + 1)
                a.copy(combT[:, half(c)], ps[0:2 * E, 6 + c, :]).then_inc(combT_ok, 1)
            with act.Fori(1, E // 2) as pair:
                e0 = pair * 2
                a.copy(b1_now[:], b1[:, bass.ds(e0, 2), :]).then_inc(b1_ok, 1)
                act.wait_ge(b1_ok, pair)
                for slot in range(2):
                    for n in range(NH):
                        for m in range(KD):
                            gelu(e0 + slot, n, m, b1_now[:, slot, :])
            for j in range(T // 2):
                act.wait_ge(mv2_ok, 2 * j + 2)
                a.activation(sd[:, 2 * j:2 * j + 2], mv[:, 2 * j:2 * j + 2, 1], ACT.Sqrt,
                             bias=eps[:]).then_inc(sd2_ok, 1)

        @block.vector
        def _(dve):
            v = nc.vector

            def x_low(c):
                cols = slice(c * 256, (c + 1) * 256)
                dve.wait_ge(xT_hi_ok, c + 1)
                v.tensor_tensor(fT_lo[:, :, cols], xT[:, :, cols], raw(fT_hi[:, :, cols]),
                                ALU.subtract).then_inc(xT_lo_ok, 1)

            def kv_out(t):
                dve.wait_ge(kv_mm, t + 1)
                v.tensor_tensor(kv[:, t, :], ps[:, t % 4, :], bkv[:], ALU.add).then_inc(kv_ok, 1)

            def kv_product(t):
                dve.wait_ge(rot_ok, t // 2 + 1)
                v.tensor_tensor(z[:, t, :], kv[:, t, 0:D], kv[:, t, D:2 * D], ALU.mult).then_inc(kv_prod, 1)

            def k_reciprocal(n):
                q4 = slice(n * TPH, (n + 1) * TPH)
                dve.wait_ge(knorm_ok, n + 1)
                v.tensor_scalar(kfloor[:, q4], knorm[:, q4], NORM_FLOOR, None, ALU.max).then_inc(kfloor_ok, 1)
                dve.wait_ge(kfloor_ok, n + 1)
                v.reciprocal(krec[:, q4], kfloor[:, q4]).then_inc(krec_ok, 1)

            dve.wait_ge(wkv_hi_ok, 1)
            v.tensor_tensor(wkv_lo[:], wkv[:], raw(wkv_hi[:]), ALU.subtract).then_inc(wkv_lo_ok, 1)
            x_low(0)
            x_low(1)
            dve.wait_ge(l_bkv, 16)
            kv_out(0)
            x_low(2)
            kv_out(1)
            x_low(3)
            kv_out(2)
            dve.wait_ge(wq_hi_ok, 1)
            v.tensor_tensor(wq_lo[:], wq[:], raw(wq_hi[:]), ALU.subtract).then_inc(wq_lo_ok, 1)
            kv_out(3)
            for t in range(4, T):
                kv_out(t)
                kv_product(t - 4)
            kv_product(4)
            kv_product(5)
            k_reciprocal(0)
            kv_product(6)
            kv_product(7)
            k_reciprocal(1)

            def q_rotate(n):
                dve.wait_ge(q_mm, 3 * n + 1)
                v.scalar_tensor_tensor(out=qa[:, n, :], in0=ps[:, (4, 7)[n], :], scalar=bq[:, 0:1],
                                       in1=rT[:, 0, half(n)], op0=ALU.add, op1=ALU.mult).then_inc(qab_ok, 1)
                dve.wait_ge(q_mm, 3 * n + 2)
                v.scalar_tensor_tensor(out=qb[:, n, :], in0=ps[:, (5, 0)[n], :], scalar=bq[:, 2:3],
                                       in1=rT[:, 1, half(n)], op0=ALU.add, op1=ALU.mult).then_inc(qab_ok, 1)

            def q_low(n):
                dve.wait_ge(q_hi_ok, n + 1)
                v.tensor_tensor(gT_lo[:, :, half(n)], qT[:, :, half(n)], raw(gT_hi[:, :, half(n)]),
                                ALU.subtract).then_inc(q_lo_ok, 1)

            dve.wait_ge(l_bq, 16)
            dve.wait_ge(l_rT, 16)
            q_rotate(0)
            dve.wait_ge(a_mm, 1)
            v.tensor_copy(acol[:], ps[:, 2:4, 0]).then_inc(acol_ok, 1)
            dve.wait_ge(l_wout, 16)
            dve.wait_ge(acol_ok, 1)
            for k in range(KD):
                v.tensor_scalar(wo_hi[:, k, :], wout[:, k, :], acol[:, k:k + 1], None,
                                ALU.mult).then_inc(wo_hi_ok, 1)
            for k in range(KD):
                dve.wait_ge(wo_hi_ok, k + 1)
                v.scalar_tensor_tensor(out=wo_lo[:, k, :], in0=wout[:, k, :], scalar=acol[:, k:k + 1],
                                       in1=raw(wo_hi[:, k, :]), op0=ALU.mult,
                                       op1=ALU.subtract).then_inc(wo_lo_ok, 1)
            q_low(0)
            q_rotate(1)
            q_low(1)

            def norm_stats(t, got, done):
                v.bn_stats(stats[:, t, :], z[:, t, :]).then_inc(got, 1)
                dve.wait_ge(got, t + 1)
                v.bn_aggr(mv[:, t, :], stats[:, t, :]).then_inc(done, 1)

            def first_sum(j):
                for t in (2 * j, 2 * j + 1):
                    dve.wait_ge(o_mm, t + 1)
                    v.tensor_tensor(z[:, t, :], ps[:, 4 + t % 4, 0:D], acc[:, t, :], ALU.add).then_inc(z_ok, 1)
                for t in (2 * j, 2 * j + 1):
                    dve.wait_ge(z_ok, t + 1)
                    norm_stats(t, stats_ok, mv_ok)

            def normalise(j, dst, roots, recs, done):
                two = slice(2 * j, 2 * j + 2)
                dve.wait_ge(roots, j + 1)
                v.reciprocal(rstd[:, two], sd[:, two]).then_inc(recs, 1)
                dve.wait_ge(recs, j + 1)
                for t in (2 * j, 2 * j + 1):
                    v.tensor_scalar(dst[:, t, :], z[:, t, :], mv[:, t, 0:1], rstd[:, t:t + 1],
                                    ALU.subtract, ALU.mult).then_inc(done, 1)

            def x1_low(t):
                dve.wait_ge(x1_hi_ok, t + 1)
                v.tensor_tensor(fT_lo[:, :, tile(t)], ps[:, 2 + t % 2, 0:D].rearrange("p (k c) -> p k c", k=KD),
                                raw(fT_hi[:, :, tile(t)]), ALU.subtract).then_inc(x1_lo_ok, 1)

            dve.wait_ge(res_ok, 1)
            first_sum(0)
            first_sum(1)
            normalise(0, x1, sd_ok, rstd_ok, x1_ok)
            first_sum(2)
            normalise(1, x1, sd_ok, rstd_ok, x1_ok)
            x1_low(0)
            x1_low(1)
            first_sum(3)
            normalise(2, x1, sd_ok, rstd_ok, x1_ok)
            x1_low(2)
            x1_low(3)
            normalise(3, x1, sd_ok, rstd_ok, x1_ok)
            for t in range(4, T):
                x1_low(t)

            def g_low(e, n, m):
                i = 2 * n + m
                dve.wait_ge(g_hi_ok, e * 4 + (i + 1))
                v.tensor_tensor(gT_lo[:, m, half(n)], h[:, i, :], raw(gT_hi[:, m, half(n)]),
                                ALU.subtract).then_inc(g_lo_ok, 1)

            def combine(e, n, first=False):
                for j in (2 * n, 2 * n + 1):
                    dve.wait_ge(y_mm, e * 4 + (j + 1))
                    if not first:
                        dve.wait_ge(y_ok, e * 4 + (j - 3))
                    for t in (2 * j, 2 * j + 1):
                        w = comb[:, t, e:e + 1] if isinstance(e, int) else comb[:, t, bass.ds(e, 1)]
                        last = v.scalar_tensor_tensor(
                            out=acc[:, t, :], in0=ps[:, 4 + j, (t % 2) * D:(t % 2 + 1) * D], scalar=w,
                            in1=(x1 if first else acc)[:, t, :], op0=ALU.mult, op1=ALU.add)
                    last.then_inc(y_ok, 1)

            g_low(0, 0, 0)
            g_low(0, 0, 1)
            g_low(0, 1, 0)

            steps = [0]

            def step(ins):
                steps[0] += 1
                ins.then_inc(route, 1)
                dve.wait_ge(route, steps[0])

            def per_tile(ap):
                return ap.unsqueeze(2).to_broadcast([P, T, E])

            order_b = order[:].unsqueeze(1).to_broadcast([P, T, E])
            dve.wait_ge(lgp_ok, 1)
            step(v.tensor_tensor(lg[:], lgp[:, :, 0:E], lgp[:, :, E:2 * E], ALU.add))

            def largest(k, src):
                step(v.reduce_max(top[:, k, :], src[:], axis=AX_X))
                step(v.tensor_tensor(hit[:], src[:], per_tile(top[:, k, :]), ALU.is_equal))
                step(v.tensor_tensor(hit[:], hit[:], order_b, ALU.mult))
                step(v.reduce_max(which[:, k, :], hit[:], axis=AX_X))
                step(v.tensor_tensor(sel[:, k, :, :], order_b, per_tile(which[:, k, :]), ALU.is_equal))

            largest(0, lg)
            step(v.scalar_tensor_tensor(out=lg2[:], in0=sel[:, 0, :, :], scalar=MASKED, in1=lg[:],
                                        op0=ALU.mult, op1=ALU.add))
            largest(1, lg2)
            v.tensor_tensor(gap[:], top[:, 0, :], top[:, 1, :], ALU.subtract).then_inc(gap_ok, 1)
            g_low(0, 1, 1)
            dve.wait_ge(th_ok, 1)
            v.tensor_scalar(wt[:, 0, :], th[:], 0.5, 0.5, ALU.mult, ALU.add)
            step(v.tensor_scalar(wt[:, 1, :], th[:], -0.5, 0.5, ALU.mult, ALU.add))
            v.tensor_tensor(hit[:], sel[:, 0, :, :], per_tile(wt[:, 0, :]), ALU.mult)
            step(v.tensor_tensor(lg2[:], sel[:, 1, :, :], per_tile(wt[:, 1, :]), ALU.mult))
            step(v.tensor_tensor(lg[:], hit[:], lg2[:], ALU.add))
            step(v.tensor_tensor(comb[:], lg[:], alp[:].unsqueeze(1).to_broadcast([P, T, E]), ALU.mult))
            step(v.tensor_copy(comb_p[:, :, 0:E].bitcast(F32R), comb[:]))
            v.tensor_tensor(comb_p[:, :, E:2 * E], comb[:], comb_p[:, :, 0:E], ALU.subtract)\
             .then_inc(comb_p_ok, 1)

            combine(0, 0, first=True)
            for m in range(KD):
                g_low(1, 0, m)
            combine(0, 1, first=True)
            for m in range(KD):
                g_low(1, 1, m)
            combine(1, 0)
            for i, j in enumerate((2, 3, 0, 1)):
                dve.wait_ge(bias_mm, i + 1)
                dve.wait_ge(y_ok, 4 + j + 1 if j < 2 else j + 1)
                for t in (2 * j, 2 * j + 1):
                    last = v.tensor_tensor(acc[:, t, :], ps[:, 4 + j, (t % 2) * D:(t % 2 + 1) * D],
                                           acc[:, t, :], ALU.add)
                last.then_inc(bias_ok, 1)
            dve.wait_ge(bias_ok, 4)
            with dve.Fori(1, E // 2) as pair:
                e0 = pair * 2
                for slot in range(2):
                    for m in range(KD):
                        g_low(e0 + slot, 0, m)
                    combine(e0 + (slot - 1), 1)
                    for m in range(KD):
                        g_low(e0 + slot, 1, m)
                    combine(e0 + slot, 0)

            def last_stats(j):
                dve.wait_ge(y_ok, 4 * (E - 1) + j + 1)
                for t in (2 * j, 2 * j + 1):
                    v.bn_stats(stats[:, t, :], acc[:, t, :]).then_inc(stats2_ok, 1)
                for t in (2 * j, 2 * j + 1):
                    dve.wait_ge(stats2_ok, t + 1)
                    v.bn_aggr(mv[:, t, :], stats[:, t, :]).then_inc(mv2_ok, 1)

            def last_norm(j):
                two = slice(2 * j, 2 * j + 2)
                dve.wait_ge(sd2_ok, j + 1)
                v.reciprocal(rstd[:, two], sd[:, two]).then_inc(rstd2_ok, 1)
                dve.wait_ge(rstd2_ok, j + 1)
                for t in (2 * j, 2 * j + 1):
                    v.tensor_scalar(z[:, t, :], acc[:, t, :], mv[:, t, 0:1], rstd[:, t:t + 1],
                                    ALU.subtract, ALU.mult).then_inc(out_ok, 1)

            last_stats(0)
            last_stats(1)
            last_norm(0)
            last_norm(1)
            combine(E - 1, 1)
            last_stats(2)
            last_stats(3)
            last_norm(2)
            last_norm(3)

        @block.tensor
        def _(pe):
            def product(dst, terms):
                for k, (lh, ll, rh, rl) in enumerate(terms):
                    nc.tensor.matmul(dst, lh, rh, start=k == 0, stop=False)
                    nc.tensor.matmul(dst, lh, rl, start=False, stop=False)
                    last = nc.tensor.matmul(dst, ll, rh, start=False, stop=k == len(terms) - 1)
                return last

            pe.wait_ge(wkv_lo_ok, 1)
            for t in range(T):
                pe.wait_ge(xT_lo_ok, t // 2 + 1)
                if t >= 4:
                    pe.wait_ge(kv_ok, t - 3)
                product(ps[:, t % 4, :], [(fT_hi[:, k, tile(t)], fT_lo[:, k, tile(t)],
                                           wkv_hi[:, k, :], wkv_lo[:, k, :]) for k in range(KD)])\
                    .then_inc(kv_mm, 1)

            def q_half(n):
                for m, bank in zip((0, 2, 1), ((4, 5, 6), (7, 0, 1))[n]):
                    if bank < 4:
                        pe.wait_ge(kv_ok, 4 + bank + 1)
                    product(ps[:, bank, :], [(wq_hi[:, k, tile(m)], wq_lo[:, k, tile(m)],
                                              fT_hi[:, k, half(n)], fT_lo[:, k, half(n)]) for k in range(KD)])\
                        .then_inc(q_mm, 1)

            pe.wait_ge(wq_lo_ok, 1)
            q_half(0)
            pe.wait_ge(kv_ok, T)
            for t in range(T):
                pe.wait_ge(kv_prod, t + 1)
                pe.wait_ge(krec_ok, t // TPH + 1)
                for k in range(KD):
                    last = nc.tensor.matmul(ps[:, 2 + k, 0:1], z[:, t, tile(k)], krec[:, t:t + 1],
                                            start=t == 0, stop=t == T - 1)
            last.then_inc(a_mm, 1)
            q_half(1)

            pe.wait_ge(wo_lo_ok, KD)
            for t in range(T):
                pe.wait_ge(q_lo_ok, t // TPH + 1)
                if t == 3:
                    pe.wait_ge(qab_ok, 3)
                if t >= 4:
                    pe.wait_ge(z_ok, t - 3)
                product(ps[:, 4 + t % 4, 0:D], [(gT_hi[:, k, tile(t)], gT_lo[:, k, tile(t)],
                                                 wo_hi[:, k, :], wo_lo[:, k, :]) for k in range(KD)])\
                    .then_inc(o_mm, 1)

            def x1_transpose(t):
                pe.wait_ge(x1_ok, t + 1)
                if t >= 2:
                    pe.wait_ge(x1_lo_ok, t - 1)
                for k in range(KD):
                    last = nc.tensor.transpose(ps[:, 2 + t % 2, tile(k)], x1[:, t, tile(k)], ident[:])
                last.then_inc(x1T_mm, 1)

            def fc1(e, slot, n):
                for m in range(KD):
                    if not isinstance(e, int) or e > 0:
                        pe.wait_ge(h_ok, e * 4 + (2 * n + m - 3))
                    product(ps[:, 2 * n + m, :],
                            [(w_hi[:, slot, k * D + m * P:k * D + (m + 1) * P],
                              w_lo[:, slot, k * D + m * P:k * D + (m + 1) * P],
                              fT_hi[:, k, half(n)], fT_lo[:, k, half(n)]) for k in range(KD)])\
                        .then_inc(fc1_mm, 1)

            def fc2(e, slot, n):
                pe.wait_ge(g_lo_ok, e * 4 + (2 * n + 2))
                for j in (2 * n, 2 * n + 1):
                    if not isinstance(e, int) or e > 0:
                        pe.wait_ge(y_ok, e * 4 + (j - 3))
                    for t in (2 * j, 2 * j + 1):
                        last = product(ps[:, 4 + j, (t % 2) * D:(t % 2 + 1) * D],
                                       [(gT_hi[:, k, tile(t)], gT_lo[:, k, tile(t)],
                                         w_hi[:, slot, (2 + k) * D:(3 + k) * D],
                                         w_lo[:, slot, (2 + k) * D:(3 + k) * D]) for k in range(KD)])
                    last.then_inc(y_mm, 1)

            pe.wait_ge(ident_ok, 1)
            for t in range(4):
                x1_transpose(t)
            pe.wait_ge(w1_ok, 1)
            pe.wait_ge(x1_lo_ok, 4)
            fc1(0, 0, 0)
            for t in range(4, T):
                x1_transpose(t)
            pe.wait_ge(gate_ok, 1)
            pe.wait_ge(x1_lo_ok, T)
            for n in range(NH):
                for k in range(KD):
                    nc.tensor.matmul(ps[:, 4 + n, :], gpad[:, k, :], fT_hi[:, k, half(n)], start=k == 0, stop=False)
                    last = nc.tensor.matmul(ps[:, 4 + n, :], gpad[:, k, :], fT_lo[:, k, half(n)],
                                            start=False, stop=k == KD - 1)
                last.then_inc(lg_mm, 1)
            fc1(0, 0, 1)
            pe.wait_ge(lgT_ok, 2)
            for t in range(T):
                last = nc.tensor.transpose(ps[:, 6, t * 2 * E:(t + 1) * 2 * E], lgT[:, tile(t)],
                                           ident[0:2 * E, 0:2 * E])
            last.then_inc(lgp_mm, 1)
            pe.wait_ge(w2_ok, 1)
            fc2(0, 0, 0)
            pe.wait_ge(w1_ok, 2)
            fc1(1, 1, 0)
            pe.wait_ge(lgp_ok, 1)
            fc2(0, 0, 1)
            fc1(1, 1, 1)
            pe.wait_ge(comb_p_ok, 1)
            pe.wait_ge(y_ok, 4)
            for t in range(T):
                last = nc.tensor.transpose(ps[0:2 * E, 6 + t // 4, tile(t % 4)], comb_p[:, t, :], ident[:])
                if t % 4 == 3:
                    last.then_inc(combT_mm, 1)
            pe.wait_ge(w2_ok, 2)
            fc2(1, 1, 0)
            pe.wait_ge(combT_ok, 2)
            pe.wait_ge(b2_ok, 1)
            for j in (2, 3, 0, 1):
                if j < 2:
                    pe.wait_ge(y_ok, 4 + j + 1)
                for t in (2 * j, 2 * j + 1):
                    dst = ps[:, 4 + j, (t % 2) * D:(t % 2 + 1) * D]
                    nc.tensor.matmul(dst, combT[:, tile(t)], b2_hi[:], start=True, stop=False)
                    last = nc.tensor.matmul(dst, combT[:, tile(t)], b2_lo[:], start=False, stop=True)
                last.then_inc(bias_mm, 1)
            with pe.Fori(1, E // 2) as pair:
                e0 = pair * 2
                for slot in range(2):
                    pe.wait_ge(w1_ok, e0 + (slot + 1))
                    fc1(e0 + slot, slot, 0)
                    pe.wait_ge(bias_ok, 4)
                    fc2(e0 + (slot - 1), 1 - slot, 1)
                    fc1(e0 + slot, slot, 1)
                    pe.wait_ge(w2_ok, e0 + (slot + 1))
                    fc2(e0 + slot, slot, 0)
            fc2(E - 1, 1, 1)


def kernel(**inputs):
    import concourse.bacc as bacc
    from concourse.bass_utils import run_bass_kernel_spmd

    a = {k.replace("L0_", ""): np.asarray(v) for k, v in inputs.items()}
    x = a["attn_X"][0]
    S, D = x.shape
    T, KD, ROT = S // P, D // P, D // 2

    def blocks(m):
        return m.reshape(-1, P, m.shape[-1]).transpose(1, 0, 2)

    w_in, b_in = a["attn_W_in"], a["attn_b_in"]
    swap = np.arange(ROT) ^ 1
    w_q = np.concatenate([w_in[:D], w_in[:ROT][swap]])
    b_q = np.concatenate([b_in[:D], b_in[:ROT][swap]]).reshape(-1, P).T

    inv_freq = (np.float32(1.0) / np.float32(ROPE_THETA) ** (np.arange(0, ROT, 2, dtype=np.float32)
                                                             / np.float32(ROT))).astype(np.float32)
    angle = np.arange(S, dtype=np.float32)[:, None] * inv_freq[None, :]
    cos, sin = np.cos(angle), np.sin(angle)
    rope_tok = np.stack([t.reshape(T, P, ROT // 2).transpose(1, 0, 2) for t in (cos, sin)], axis=1)
    sign = np.where(np.arange(ROT) % 2 == 0, -1.0, 1.0).astype(np.float32)
    rope_t = np.stack([np.repeat(cos, 2, axis=1).T, np.repeat(sin, 2, axis=1).T * sign[:, None]], axis=1)

    E = a["ffn_gate_w"].shape[1]
    experts = np.concatenate([a["ffn_fc1_w"].reshape(E, KD, P, D), a["ffn_fc2_w"].reshape(E, KD, P, D)],
                             axis=1).transpose(0, 2, 1, 3).reshape(E, P, 4 * D)
    arrays = {
        "x_tok": x.reshape(T, P, D).transpose(1, 0, 2),
        "x_t": blocks(x.T),
        "w_kv_t": blocks(w_in[D:].T),
        "w_q_t": blocks(w_q.T),
        "w_out_t": blocks(a["attn_W_out"].T),
        "b_kv": b_in[D:],
        "b_q": b_q,
        "b_out": a["attn_b_out"],
        "rope_tok": rope_tok,
        "rope_t": rope_t,
        "gate_w": blocks(a["ffn_gate_w"]),
        "expert_w": experts,
        "fc1_b": a["ffn_fc1_b"].reshape(E, KD, P).transpose(2, 0, 1),
        "fc2_b": np.concatenate([a["ffn_fc2_b"]] * 2),
        "alpha": a["ffn_alpha"],
        "tie_order": np.arange(E, 0, -1).astype(np.float32),
    }
    nc = bacc.Bacc("TRN2", target_bir_lowering=False, num_devices=1)
    send, args = {}, []
    for name, value in arrays.items():
        value = np.ascontiguousarray(value)
        send[f"in_{name}"] = value
        args.append(nc.dram_tensor(f"in_{name}", value.shape, F32, kind="ExternalInput").ap())
    out = nc.dram_tensor("out", (S, D), F32, kind="ExternalOutput")
    layer_kernel(nc, *args, out.ap())
    result = run_bass_kernel_spmd(nc, [send], core_ids=[0])
    return result.results[0]["out"].reshape(1, S, D)
```

```python
from contextlib import ExitStack

import numpy as np

import concourse.bass as bass
from concourse import mybir

ALU = mybir.AluOpType
ACT = mybir.ActivationFunctionType
AX_X = mybir.AxisListType.X
F32 = mybir.dt.float32
F32R = mybir.dt.float32r

P = 128
ROPE_THETA = 10000.0
LN_EPS = 1e-5
NORM_FLOOR = 1e-12
MASKED = -3.0e38
WARM_LOADS = 16
WARM_NORM = 5


def layer_kernel(nc, x_tok, x_t, w_kv_t, w_q_t, w_out_t, b_rows, rope_tok, rope_t,
                 columns, expert_w, fc2_b, out):
    _, T, D = x_tok.shape
    S = T * P
    KD = D // P
    E = expert_w.shape[0]
    ROT = 2 * rope_tok.shape[-1]
    HALF = rope_tok.shape[-1]
    NH = S // 512
    TPH = T // NH
    assert (D, KD, NH, E, T) == (256, 2, 2, 8, 8)

    with ExitStack() as ctx:
        def sb(name, shape, dt=F32):
            return ctx.enter_context(nc.sbuf_tensor(name, shape, dt))

        def sem(name):
            return ctx.enter_context(nc.semaphore(name))

        ps = ctx.enter_context(nc.psum_tensor("ps", [P, 8, 512], F32))

        xT = sb("xT", [P, KD, S])
        wkv = sb("wkv", [P, KD, 2 * D])
        wq = sb("wq", [P, KD, D + ROT])
        wout = sb("wout", [P, KD, D])
        brow = sb("brow", [P, 3 * D])
        bkv, bout = brow[:, 0:2 * D], brow[:, 2 * D:3 * D]
        rtok = sb("rtok", [P, 2, T, HALF])
        rT = sb("rT", [P, 2, S])
        wraw = sb("wraw", [P, 2, 4 * D])
        cols = sb("cols", [P, columns.shape[1]])
        bq = cols[:, 0:3]
        gw = cols[:, 3:3 + KD * E].rearrange("p (k e) -> p k e", k=KD)
        b1 = cols[:, 3 + KD * E:3 + 2 * KD * E].rearrange("p (e k) -> p e k", k=KD)
        alp = cols[:, 3 + 2 * KD * E:3 + 2 * KD * E + E]
        order = cols[:, 3 + 2 * KD * E + E:3 + 2 * KD * E + 2 * E]
        b1_now = sb("b1_now", [P, 2, KD])
        b2 = sb("b2", [2 * E, D])

        fT_hi = sb("fT_hi", [P, KD, S], F32R)
        fT_lo = sb("fT_lo", [P, KD, S], F32R)
        wkv_hi = sb("wkv_hi", [P, KD, 2 * D], F32R)
        wkv_lo = sb("wkv_lo", [P, KD, 2 * D], F32R)
        wq_hi = sb("wq_hi", [P, KD, D + ROT], F32R)
        wq_lo = sb("wq_lo", [P, KD, D + ROT], F32R)
        kv = sb("kv", [P, T, 2 * D])
        ksq = sb("ksq", [P, T])
        knorm = sb("knorm", [P, T])
        kfloor = sb("kfloor", [P, T])
        krec = sb("krec", [P, T])
        acol = sb("acol", [P, KD])
        wo_hi = sb("wo_hi", [P, KD, D], F32R)
        wo_lo = sb("wo_lo", [P, KD, D], F32R)
        qa = sb("qa", [P, NH, 512])
        qb = sb("qb", [P, NH, 512])
        qT = sb("qT", [P, KD, S])
        gT_hi = sb("gT_hi", [P, KD, S], F32R)
        gT_lo = sb("gT_lo", [P, KD, S], F32R)

        z = sb("z", [P, T, D])
        acc = sb("acc", [P, T, D])
        x1 = sb("x1", [P, T, D])
        rot_a, rot_b = (x1[:, i * T // 2:(i + 1) * T // 2, :].rearrange("p t (u r) -> p (t u) r", r=ROT)
                        for i in range(2))
        stats = sb("stats", [P, T, 6])
        mv = sb("mv", [P, T, 2])
        sd = sb("sd", [P, T])
        sd_unused = sb("sd_unused", [P, 1])
        rstd = sb("rstd", [P, T])
        shift = sb("shift", [P, T])
        ident = sb("ident", [P, P])
        eps = sb("eps", [P, 1])
        zero = sb("zero", [P, 1])

        gpad = sb("gpad", [P, KD, P], F32R)
        lgT = sb("lgT", [2 * E, S])
        lgp = sb("lgp", [P, T, 2 * E])
        lg = sb("lg", [P, T, E])
        lg2 = sb("lg2", [P, T, E])
        hit = sb("hit", [P, T, E])
        sel = sb("sel", [P, 2, T, E])
        top = sb("top", [P, 2, T])
        which = sb("which", [P, 2, T])
        gap = sb("gap", [P, T])
        th = sb("th", [P, T])
        wt = sb("wt", [P, 2, T])
        comb = sb("comb", [P, T, E])
        comb_p = sb("comb_p", [P, T, 2 * E])
        combT = sb("combT", [2 * E, S], F32R)
        b2_hi = sb("b2_hi", [2 * E, D], F32R)
        b2_lo = sb("b2_lo", [2 * E, D], F32R)

        w_hi = sb("w_hi", [P, 2, 4 * D], F32R)
        w_lo = sb("w_lo", [P, 2, 4 * D], F32R)
        h = kv[:, 0:2 * NH, :]

        l_wq, l_wout, l_brow, l_rtok, l_rT, l_cols, l_b2, l_x = (
            sem(f"l_{n}") for n in "wq wout brow rtok rT cols b2 x".split())
        l_wkv = [sem(f"l_wkv{k}") for k in range(KD)]
        l_xT = [sem(f"l_xT{c}") for c in range(4)]
        l_exp = [sem(f"l_exp{slot}") for slot in range(2)]
        stored = sem("stored")
        wkv_hi_ok, wkv_lo_ok, xT_hi_ok, xT_lo_ok, wq_hi_ok, wq_lo_ok = (
            sem(n) for n in "wkv_hi_ok wkv_lo_ok xT_hi_ok xT_lo_ok wq_hi_ok wq_lo_ok".split())
        kv_mm, kv_ok, rot_parts, rot_ok, vrot_parts, vrot_ok, kv_prod, ksq_ok, knorm_ok, kfloor_ok, krec_ok = (
            sem(n) for n in "kv_mm kv_ok rot_parts rot_ok vrot_parts vrot_ok kv_prod ksq_ok knorm_ok kfloor_ok krec_ok".split())
        q_mm, qab_ok, q_rot_ok, q_pass_ok, q_hi_ok, q_rot_lo_ok, q_pass_lo_ok = (
            sem(n) for n in "q_mm qab_ok q_rot_ok q_pass_ok q_hi_ok q_rot_lo_ok q_pass_lo_ok".split())
        a_mm, acol_ok, wo_hi_ok, wo_lo_ok = (sem(n) for n in "a_mm acol_ok wo_hi_ok wo_lo_ok".split())
        o_mm, res_dbl, res_ok, z_ok, stats_ok, mv_ok, sd_ok, rstd_ok, shift_ok, x1_ok, x1T_mm, x1_hi_ok, x1_lo_ok = (
            sem(n) for n in "o_mm res_dbl res_ok z_ok stats_ok mv_ok sd_ok rstd_ok shift_ok x1_ok x1T_mm x1_hi_ok x1_lo_ok".split())
        ident0, ident_ok, gpad0, gate_hi_ok, gate_ok, b2_hi_ok, b2_ok = (
            sem(n) for n in "ident0 ident_ok gpad0 gate_hi_ok gate_ok b2_hi_ok b2_ok".split())
        lg_mm, lgT_ok, lgp_mm, lgp_ok, route, gap_ok, th_ok, comb_p_ok, combT_mm, combT_ok, bias_mm, bias_ok = (
            sem(n) for n in "lg_mm lgT_ok lgp_mm lgp_ok route gap_ok th_ok comb_p_ok combT_mm combT_ok bias_mm bias_ok".split())
        const_ok, b1_ok, w_part, w1_ok, w2_ok, h_ok, g_hi_ok, g_lo_ok, y_mm, y_ok = (
            sem(n) for n in "const_ok b1_ok w_part w1_ok w2_ok h_ok g_hi_ok g_lo_ok y_mm y_ok".split())
        fc1_mm = [sem(f"fc1_mm{n}") for n in range(NH)]
        stats2_ok, mv2_ok, sd2_ok, rstd2_ok, shift2_ok, out_ok, out_dve_ok, y_scaled, last_sum = (
            sem(n) for n in "stats2_ok mv2_ok sd2_ok rstd2_ok shift2_ok out_ok out_dve_ok y_scaled last_sum".split())

        def raw(part):
            return part.bitcast(F32)

        def half(n):
            return slice(n * 512, (n + 1) * 512)

        def tile(t):
            return slice(t * P, (t + 1) * P)

        POOL_ROTATES = ((0, 2), (2, 3), (4, 6), (6, 7))
        DVE_ROTATES = (3, 7)

        def pairs(ap):
            return ap.rearrange("p t (i c) -> p t i c", c=2)

        def rotary_product(t0, t1, part, c):
            tiles = slice(t0, t1)
            return (pairs((rot_a, rot_b)[part][:, tiles, :])[:, :, :, c],
                    pairs(kv[:, tiles, 0:ROT])[:, :, :, c if part == 0 else 1 - c], rtok[:, part, tiles, :])

        def rotary_sum(t0, t1, c):
            tiles = slice(t0, t1)
            return (pairs(kv[:, tiles, 0:ROT])[:, :, :, c], pairs(rot_a[:, tiles, :])[:, :, :, c],
                    pairs(rot_b[:, tiles, :])[:, :, :, c])

        X1T_BANK = (2, 3, 0, 2, 4, 5, 6, 7)

        block = ctx.enter_context(nc.Block())

        @block.sync
        def _(sp):
            def load_x_t(c):
                part = slice(c * 256, (c + 1) * 256)
                sp.dma_start(xT[:, :, part], x_t[:, :, part]).then_inc(l_xT[c], 16)

            sp.dma_start(wkv[:, 0, :], w_kv_t[:, 0, :]).then_inc(l_wkv[0], 16)
            load_x_t(0)
            sp.dma_start(wkv[:, 1, :], w_kv_t[:, 1, :]).then_inc(l_wkv[1], 16)
            load_x_t(1)
            sp.dma_start(brow[:], b_rows.partition_broadcast(P)).then_inc(l_brow, 16)
            load_x_t(2)
            load_x_t(3)
            sp.dma_start(rtok[:], rope_tok).then_inc(l_rtok, 16)
            sp.dma_start(wq[:], w_q_t).then_inc(l_wq, 16)
            sp.dma_start(acc[:], x_tok).then_inc(l_x, 16)
            sp.dma_start(cols[:], columns).then_inc(l_cols, 16)
            sp.dma_start(rT[:], rope_t).then_inc(l_rT, 16)
            sp.dma_start(wout[:], w_out_t).then_inc(l_wout, 16)
            sp.dma_start(b2[:], fc2_b).then_inc(l_b2, 16)
            for e in range(2):
                sp.dma_start(wraw[:, e, :], expert_w[e]).then_inc(l_exp[e], 16)
            with sp.Fori(1, E // 2) as pair:
                for slot in range(2):
                    sp.wait_ge(w2_ok, pair * 2 + (slot - 1))
                    sp.dma_start(wraw[:, slot, :], expert_w[bass.ds(pair * 2 + slot, 1)].squeeze(0))\
                      .then_inc(l_exp[slot], 16)
            for j in range(T // 2):
                if j < T // 2 - 1:
                    sp.wait_ge(out_ok, 2 * j + 2)
                else:
                    sp.wait_ge(out_dve_ok, 2)
                sp.dma_start(out[2 * j * P:(2 * j + 2) * P, :].rearrange("(t p) d -> p t d", p=P),
                             z[:, 2 * j:2 * j + 2, :]).then_inc(stored, 16)
            sp.wait_ge(stored, 16 * (T // 2))

        @block.gpsimd
        def _(pool):
            g = nc.gpsimd
            g.memset(ident[:], 0.0).then_inc(ident0, 1)
            g.memset(zero[:], 0.0).then_inc(const_ok, 1)
            g.memset(eps[:], LN_EPS).then_inc(const_ok, 1)
            g.memset(raw(gpad[:]), 0.0).then_inc(gpad0, 1)
            pool.wait_ge(ident0, 1)
            g.affine_select(out=ident[:], in_=ident[:], compare_op=ALU.not_equal, fill=1.0, base=0,
                            pattern=[[-1, P]], channel_multiplier=1).then_inc(ident_ok, 1)
            pool.wait_ge(l_rtok, 16)
            for i, (t0, t1) in enumerate(POOL_ROTATES):
                pool.wait_ge(kv_ok, t1)
                for c in range(2):
                    g.tensor_tensor(*rotary_product(t0, t1, 0, c), ALU.mult)
                    g.tensor_tensor(*rotary_product(t0, t1, 1, c), ALU.mult).then_inc(rot_parts, 1)
                pool.wait_ge(rot_parts, 2 * i + 2)
                pool.wait_ge(ksq_ok, t1)
                g.tensor_tensor(*rotary_sum(t0, t1, 0), ALU.subtract)
                g.tensor_tensor(*rotary_sum(t0, t1, 1), ALU.add).then_inc(rot_ok, 1)
            pool.wait_ge(l_brow, 16)
            for n in range(NH):
                pool.wait_ge(res_dbl, n + 1)
                four = slice(n * TPH, (n + 1) * TPH)
                g.tensor_tensor(acc[:, four, :], acc[:, four, :], bout.unsqueeze(1).to_broadcast([P, TPH, D]),
                                ALU.add).then_inc(res_ok, 1)
            for n in range(NH):
                pool.wait_ge(q_hi_ok, 2 * n + 1)
                g.tensor_tensor(gT_lo[:, 1, half(n)], qT[:, 1, half(n)], raw(gT_hi[:, 1, half(n)]),
                                ALU.subtract).then_inc(q_pass_lo_ok, 1)
            pool.wait_ge(l_cols, 16)
            pool.wait_ge(gpad0, 1)
            g.tensor_copy(gpad[:, :, 0:E], gw).then_inc(gate_hi_ok, 1)
            pool.wait_ge(l_b2, 16)
            g.tensor_copy(b2_hi[:], b2[:]).then_inc(b2_hi_ok, 1)
            pool.wait_ge(gate_hi_ok, 1)
            g.tensor_tensor(gpad[:, :, E:2 * E], gw, raw(gpad[:, :, 0:E]), ALU.subtract).then_inc(gate_ok, 1)
            pool.wait_ge(b2_hi_ok, 1)
            g.tensor_tensor(b2_lo[:], b2[:], raw(b2_hi[:]), ALU.subtract).then_inc(b2_ok, 1)

            def split(slot, part, n_parts, ok):
                cols = slice(part * 2 * D, (part + 1) * 2 * D)
                src = wraw[:, slot, cols]
                g.tensor_tensor(w_hi[:, slot, cols], src, zero[:].to_broadcast([P, 2 * D]),
                                ALU.add).then_inc(w_part, 1)
                pool.wait_ge(w_part, n_parts)
                g.tensor_tensor(w_lo[:, slot, cols], src, raw(w_hi[:, slot, cols]), ALU.subtract).then_inc(ok, 1)

            pool.wait_ge(const_ok, 1)
            for e in range(2):
                pool.wait_ge(l_exp[e], 16)
                split(e, 0, 2 * e + 1, w1_ok)
                split(e, 1, 2 * e + 2, w2_ok)
            with pool.Fori(1, E // 2) as pair:
                e0 = pair * 2
                for slot in range(2):
                    pool.wait_ge(l_exp[slot], pair * 16 + 16)
                    pool.wait_ge(fc1_mm[1], e0 * 2 + (2 * slot - 2))
                    split(slot, 0, e0 * 2 + (2 * slot + 1), w1_ok)
                    pool.wait_ge(y_mm, e0 * 4 + (4 * slot - 4))
                    split(slot, 1, e0 * 2 + (2 * slot + 2), w2_ok)

            pool.wait_ge(y_ok, 4 * (E - 2) + 2)
            for t in (2, 3):
                pool.wait_ge(y_scaled, t - 1)
                g.tensor_tensor(acc[:, t, :], acc[:, t, :], x1[:, t, :], ALU.add).then_inc(last_sum, 1)

        @block.scalar
        def _(act):
            a = nc.scalar
            def x_high(c):
                part = slice(c * 256, (c + 1) * 256)
                act.wait_ge(l_xT[c], 16)
                a.copy(fT_hi[:, :, part], xT[:, :, part]).then_inc(xT_hi_ok, 1)

            for k in range(KD):
                act.wait_ge(l_wkv[k], 16)
                a.copy(wkv_hi[:, k, :], wkv[:, k, :]).then_inc(wkv_hi_ok, 1)
                x_high(k)
            x_high(2)
            x_high(3)
            act.wait_ge(l_wq, 16)
            a.copy(wq_hi[:], wq[:]).then_inc(wq_hi_ok, 1)
            for t in range(T):
                act.wait_ge(kv_ok, t + 1)
                a.activation(gT_lo[:, t // TPH, (t % TPH) * D:(t % TPH + 1) * D], kv[:, t, 0:D], ACT.Square,
                             accum_out=ksq[:, t:t + 1]).then_inc(ksq_ok, 1)
                if t % TPH == TPH - 1:
                    act.wait_ge(ksq_ok, t + 1)
                    q4 = slice(t - TPH + 1, t + 1)
                    a.activation(knorm[:, q4], ksq[:, q4], ACT.Sqrt).then_inc(knorm_ok, 1)
                if t in (3, 5):
                    if t == 3:
                        act.wait_ge(l_x, 16)
                    four = slice((t - 3) // 2 * TPH, ((t - 3) // 2 + 1) * TPH)
                    a.mul(acc[:, four, :], acc[:, four, :], 2.0).then_inc(res_dbl, 1)
            act.wait_ge(l_cols, 16)
            for n in range(NH):
                act.wait_ge(q_mm, 3 * n + 3)
                a.activation(qT[:, 1, half(n)], ps[:, (6, 1)[n], :], ACT.Identity,
                             bias=bq[:, 1:2]).then_inc(q_pass_ok, 1)
                act.wait_ge(q_pass_ok, n + 1)
                a.copy(gT_hi[:, 1, half(n)], qT[:, 1, half(n)]).then_inc(q_hi_ok, 1)
                act.wait_ge(q_rot_ok, n + 1)
                a.copy(gT_hi[:, 0, half(n)], qT[:, 0, half(n)]).then_inc(q_hi_ok, 1)

            def root(j):
                act.wait_ge(mv_ok, 2 * j + 2)
                a.activation(sd[:, 2 * j:2 * j + 2], mv[:, 2 * j:2 * j + 2, 1], ACT.Sqrt,
                             bias=eps[:]).then_inc(sd_ok, 1)

            def x1_high(t):
                act.wait_ge(x1T_mm, t + 1)
                a.copy(fT_hi[:, :, tile(t)], ps[:, X1T_BANK[t], 0:D].rearrange("p (k c) -> p k c", k=KD))\
                 .then_inc(x1_hi_ok, 1)

            act.wait_ge(const_ok, 2)
            def normalise(j, src, dst, shifts, done):
                act.wait_ge(shifts, j + 1)
                for t in (2 * j, 2 * j + 1):
                    a.activation(dst[:, t, :], src[:, t, :], ACT.Identity, scale=rstd[:, t:t + 1],
                                 bias=shift[:, t:t + 1]).then_inc(done, 1)

            root(0)
            normalise(0, z, x1, shift_ok, x1_ok)
            for j in range(1, T // 2):
                root(j)
                if j < T // 2 - 1:
                    x1_high(2 * j - 2)
                    x1_high(2 * j - 1)
                normalise(j, z, x1, shift_ok, x1_ok)
            def gelu(e, n, m, bias):
                i = 2 * n + m
                act.wait_ge(fc1_mm[n], e * 2 + (m + 1))
                if not isinstance(e, int) or e > 0:
                    act.wait_ge(g_lo_ok, e * 4 + (i - 3))
                a.activation(h[:, i, :], ps[:, i, :], ACT.Gelu, bias=bias[:, m:m + 1]).then_inc(h_ok, 1)
                act.wait_ge(h_ok, e * 4 + (i + 1))
                a.copy(gT_hi[:, m, half(n)], h[:, i, :]).then_inc(g_hi_ok, 1)

            for t in range(4, T):
                x1_high(t)
            gelu(0, 0, 0, b1[:, 0, :])
            gelu(0, 0, 1, b1[:, 0, :])
            for n in range(NH):
                act.wait_ge(lg_mm, n + 1)
                a.copy(lgT[:, half(n)], ps[0:2 * E, 4 + n, :]).then_inc(lgT_ok, 1)
            gelu(0, 1, 0, b1[:, 0, :])
            act.wait_ge(lgp_mm, 1)
            a.copy(lgp[:], ps[:, 6, 0:T * 2 * E].rearrange("p (t c) -> p t c", t=T)).then_inc(lgp_ok, 1)
            gelu(0, 1, 1, b1[:, 0, :])
            act.wait_ge(gap_ok, 1)
            a.activation(th[:], gap[:], ACT.Tanh, scale=0.5).then_inc(th_ok, 1)
            for n in range(NH):
                for m in range(KD):
                    gelu(1, n, m, b1[:, 1, :])
            for c in range(2):
                act.wait_ge(combT_mm, c + 1)
                a.copy(combT[:, half(c)], ps[0:2 * E, 6 + c, :]).then_inc(combT_ok, 1)
            with act.Fori(1, E // 2) as pair:
                e0 = pair * 2
                a.copy(b1_now[:], b1[:, bass.ds(e0, 2), :]).then_inc(b1_ok, 1)
                act.wait_ge(b1_ok, pair)
                for slot in range(2):
                    for n in range(NH):
                        for m in range(KD):
                            gelu(e0 + slot, n, m, b1_now[:, slot, :])
            a.activation(sd_unused[:], eps[:], ACT.Sqrt)
            for t in (2, 3):
                act.wait_ge(y_mm, 4 * (E - 1) + t // 2 + 1)
                a.activation(x1[:, t, :], ps[:, 4 + t // 2, (t % 2) * D:(t % 2 + 1) * D], ACT.Copy,
                             scale=comb[:, t, E - 1:E]).then_inc(y_scaled, 1)

            def root2(j):
                act.wait_ge(mv2_ok, 2 * j + 2)
                a.activation(sd[:, 2 * j:2 * j + 2], mv[:, 2 * j:2 * j + 2, 1], ACT.Sqrt,
                             bias=eps[:]).then_inc(sd2_ok, 1)

            root2(0)
            normalise(0, acc, z, shift2_ok, out_ok)
            root2(1)
            root2(2)
            normalise(1, acc, z, shift2_ok, out_ok)
            root2(3)
            normalise(2, acc, z, shift2_ok, out_ok)

        @block.vector
        def _(dve):
            v = nc.vector

            def kv_low(k):
                dve.wait_ge(wkv_hi_ok, k + 1)
                v.tensor_tensor(wkv_lo[:, k, :], wkv[:, k, :], raw(wkv_hi[:, k, :]),
                                ALU.subtract).then_inc(wkv_lo_ok, 1)

            def x_low(c):
                part = slice(c * 256, (c + 1) * 256)
                dve.wait_ge(xT_hi_ok, c + 1)
                v.tensor_tensor(fT_lo[:, :, part], xT[:, :, part], raw(fT_hi[:, :, part]),
                                ALU.subtract).then_inc(xT_lo_ok, 1)

            def kv_out(t):
                dve.wait_ge(kv_mm, t + 1)
                v.tensor_tensor(kv[:, t, :], ps[:, t % 4, :], bkv, ALU.add).then_inc(kv_ok, 1)

            def rotate(t):
                i = DVE_ROTATES.index(t)
                dve.wait_ge(kv_ok, t + 1)
                for c in range(2):
                    v.tensor_tensor(*rotary_product(t, t + 1, 0, c), ALU.mult)
                    v.tensor_tensor(*rotary_product(t, t + 1, 1, c), ALU.mult).then_inc(vrot_parts, 1)
                dve.wait_ge(vrot_parts, 2 * i + 2)
                dve.wait_ge(ksq_ok, t + 1)
                v.tensor_tensor(*rotary_sum(t, t + 1, 0), ALU.subtract)
                v.tensor_tensor(*rotary_sum(t, t + 1, 1), ALU.add).then_inc(vrot_ok, 1)

            def kv_product(t):
                if t in DVE_ROTATES:
                    dve.wait_ge(vrot_ok, DVE_ROTATES.index(t) + 1)
                else:
                    dve.wait_ge(rot_ok, [t < t1 for _, t1 in POOL_ROTATES].index(True) + 1)
                v.tensor_tensor(z[:, t, :], kv[:, t, 0:D], kv[:, t, D:2 * D], ALU.mult).then_inc(kv_prod, 1)

            def k_reciprocal(n):
                q4 = slice(n * TPH, (n + 1) * TPH)
                dve.wait_ge(knorm_ok, n + 1)
                v.tensor_scalar(kfloor[:, q4], knorm[:, q4], NORM_FLOOR, None, ALU.max).then_inc(kfloor_ok, 1)
                dve.wait_ge(kfloor_ok, n + 1)
                v.reciprocal(krec[:, q4], kfloor[:, q4]).then_inc(krec_ok, 1)

            kv_low(0)
            x_low(0)
            kv_low(1)
            x_low(1)
            dve.wait_ge(l_brow, 16)
            kv_out(0)
            x_low(2)
            kv_out(1)
            x_low(3)
            kv_out(2)
            kv_out(3)
            dve.wait_ge(l_rtok, 16)
            rotate(3)
            kv_out(4)
            dve.wait_ge(wq_hi_ok, 1)
            v.tensor_tensor(wq_lo[:], wq[:], raw(wq_hi[:]), ALU.subtract).then_inc(wq_lo_ok, 1)
            kv_product(0)
            kv_out(5)
            kv_product(1)
            kv_product(2)
            kv_out(6)
            kv_product(3)
            k_reciprocal(0)
            kv_out(7)
            rotate(7)
            k_reciprocal(1)
            for t in range(4, T):
                kv_product(t)

            def q_rotate(n):
                dve.wait_ge(q_mm, 3 * n + 1)
                v.scalar_tensor_tensor(out=qa[:, n, :], in0=ps[:, (4, 7)[n], :], scalar=bq[:, 0:1],
                                       in1=rT[:, 0, half(n)], op0=ALU.add, op1=ALU.mult).then_inc(qab_ok, 1)
                dve.wait_ge(q_mm, 3 * n + 2)
                v.scalar_tensor_tensor(out=qb[:, n, :], in0=ps[:, (5, 0)[n], :], scalar=bq[:, 2:3],
                                       in1=rT[:, 1, half(n)], op0=ALU.add, op1=ALU.mult).then_inc(qab_ok, 1)

                dve.wait_ge(qab_ok, 2 * n + 2)
                v.tensor_tensor(qT[:, 0, half(n)], qa[:, n, :], qb[:, n, :], ALU.add).then_inc(q_rot_ok, 1)

            def q_low(n):
                dve.wait_ge(q_hi_ok, 2 * n + 2)
                v.tensor_tensor(gT_lo[:, 0, half(n)], qT[:, 0, half(n)], raw(gT_hi[:, 0, half(n)]),
                                ALU.subtract).then_inc(q_rot_lo_ok, 1)

            dve.wait_ge(l_cols, 16)
            dve.wait_ge(l_rT, 16)
            q_rotate(0)
            q_low(0)
            dve.wait_ge(a_mm, 1)
            v.tensor_copy(acol[:], ps[:, 2:4, 0]).then_inc(acol_ok, 1)
            dve.wait_ge(l_wout, 16)
            dve.wait_ge(acol_ok, 1)
            for k in range(KD):
                v.tensor_scalar(wo_hi[:, k, :], wout[:, k, :], acol[:, k:k + 1], None,
                                ALU.mult).then_inc(wo_hi_ok, 1)
            for k in range(KD):
                dve.wait_ge(wo_hi_ok, k + 1)
                v.scalar_tensor_tensor(out=wo_lo[:, k, :], in0=wout[:, k, :], scalar=acol[:, k:k + 1],
                                       in1=raw(wo_hi[:, k, :]), op0=ALU.mult,
                                       op1=ALU.subtract).then_inc(wo_lo_ok, 1)
            q_rotate(1)

            def first_sum(j):
                for t in (2 * j, 2 * j + 1):
                    dve.wait_ge(o_mm, t + 1)
                    v.tensor_tensor(z[:, t, :], ps[:, 4 + t % 4, 0:D], acc[:, t, :], ALU.add).then_inc(z_ok, 1)

            def first_stats(j):
                for t in (2 * j, 2 * j + 1):
                    dve.wait_ge(z_ok, t + 1)
                    v.bn_stats(stats[:, t, :], z[:, t, :]).then_inc(stats_ok, 1)
                for t in (2 * j, 2 * j + 1):
                    dve.wait_ge(stats_ok, t + 1)
                    v.bn_aggr(mv[:, t, :], stats[:, t, :]).then_inc(mv_ok, 1)

            def norm_scales(j, roots, recs, done):
                two = slice(2 * j, 2 * j + 2)
                dve.wait_ge(roots, j + 1)
                v.reciprocal(rstd[:, two], sd[:, two]).then_inc(recs, 1)
                dve.wait_ge(recs, j + 1)
                v.scalar_tensor_tensor(out=shift[:, two], in0=mv[:, two, 0], scalar=-1.0, in1=rstd[:, two],
                                       op0=ALU.mult, op1=ALU.mult).then_inc(done, 1)

            def x1_low(t):
                dve.wait_ge(x1_hi_ok, t + 1)
                v.tensor_tensor(fT_lo[:, :, tile(t)], ps[:, X1T_BANK[t], 0:D].rearrange("p (k c) -> p k c", k=KD),
                                raw(fT_hi[:, :, tile(t)]), ALU.subtract).then_inc(x1_lo_ok, 1)

            dve.wait_ge(res_ok, 1)
            first_sum(0)
            q_low(1)
            first_stats(0)
            first_sum(1)
            first_stats(1)
            norm_scales(0, sd_ok, rstd_ok, shift_ok)
            dve.wait_ge(res_ok, 2)
            for j in range(2, T // 2):
                first_sum(j)
                first_stats(j)
                norm_scales(j - 1, sd_ok, rstd_ok, shift_ok)
                x1_low(2 * j - 4)
                x1_low(2 * j - 3)
            norm_scales(T // 2 - 1, sd_ok, rstd_ok, shift_ok)
            for t in range(4, T):
                x1_low(t)

            def g_low(e, n, m):
                i = 2 * n + m
                dve.wait_ge(g_hi_ok, e * 4 + (i + 1))
                v.tensor_tensor(gT_lo[:, m, half(n)], h[:, i, :], raw(gT_hi[:, m, half(n)]),
                                ALU.subtract).then_inc(g_lo_ok, 1)

            def combine_pair(e, j, first=False):
                dve.wait_ge(y_mm, e * 4 + (j + 1))
                if not first:
                    dve.wait_ge(y_ok, e * 4 + (j - 3))
                for t in (2 * j, 2 * j + 1):
                    w = comb[:, t, e:e + 1] if isinstance(e, int) else comb[:, t, bass.ds(e, 1)]
                    last = v.scalar_tensor_tensor(
                        out=acc[:, t, :], in0=ps[:, 4 + j, (t % 2) * D:(t % 2 + 1) * D], scalar=w,
                        in1=(x1 if first else acc)[:, t, :], op0=ALU.mult, op1=ALU.add)
                last.then_inc(y_ok, 1)

            def combine(e, n, first=False):
                combine_pair(e, 2 * n, first)
                combine_pair(e, 2 * n + 1, first)

            g_low(0, 0, 0)
            g_low(0, 0, 1)
            g_low(0, 1, 0)

            steps = [0]

            def step(ins):
                steps[0] += 1
                ins.then_inc(route, 1)
                dve.wait_ge(route, steps[0])

            def per_tile(ap):
                return ap.unsqueeze(2).to_broadcast([P, T, E])

            order_b = order.unsqueeze(1).to_broadcast([P, T, E])
            dve.wait_ge(lgp_ok, 1)
            step(v.tensor_tensor(lg[:], lgp[:, :, 0:E], lgp[:, :, E:2 * E], ALU.add))

            def largest(k, src):
                step(v.reduce_max(top[:, k, :], src[:], axis=AX_X))
                step(v.tensor_tensor(hit[:], src[:], per_tile(top[:, k, :]), ALU.is_equal))
                step(v.tensor_tensor(hit[:], hit[:], order_b, ALU.mult))
                step(v.reduce_max(which[:, k, :], hit[:], axis=AX_X))
                step(v.tensor_tensor(sel[:, k, :, :], order_b, per_tile(which[:, k, :]), ALU.is_equal))

            largest(0, lg)
            g_low(0, 1, 1)
            step(v.scalar_tensor_tensor(out=lg2[:], in0=sel[:, 0, :, :], scalar=MASKED, in1=lg[:],
                                        op0=ALU.mult, op1=ALU.add))
            largest(1, lg2)
            v.tensor_tensor(gap[:], top[:, 0, :], top[:, 1, :], ALU.subtract).then_inc(gap_ok, 1)
            dve.wait_ge(th_ok, 1)
            v.tensor_scalar(wt[:, 0, :], th[:], 0.5, 0.5, ALU.mult, ALU.add)
            step(v.tensor_scalar(wt[:, 1, :], th[:], -0.5, 0.5, ALU.mult, ALU.add))
            v.tensor_tensor(hit[:], sel[:, 0, :, :], per_tile(wt[:, 0, :]), ALU.mult)
            step(v.tensor_tensor(lg2[:], sel[:, 1, :, :], per_tile(wt[:, 1, :]), ALU.mult))
            step(v.tensor_tensor(lg[:], hit[:], lg2[:], ALU.add))
            step(v.tensor_tensor(comb[:], lg[:], alp.unsqueeze(1).to_broadcast([P, T, E]), ALU.mult))
            step(v.tensor_copy(comb_p[:, :, 0:E].bitcast(F32R), comb[:]))
            v.tensor_tensor(comb_p[:, :, E:2 * E], comb[:], comb_p[:, :, 0:E], ALU.subtract)\
             .then_inc(comb_p_ok, 1)

            combine(0, 0, first=True)
            combine(0, 1, first=True)
            for m in range(KD):
                g_low(1, 0, m)
            for m in range(KD):
                g_low(1, 1, m)
            combine(1, 0)
            for i, j in enumerate((2, 3, 0, 1)):
                dve.wait_ge(bias_mm, i + 1)
                dve.wait_ge(y_ok, 4 + j + 1 if j < 2 else j + 1)
                for t in (2 * j, 2 * j + 1):
                    last = v.tensor_tensor(acc[:, t, :], ps[:, 4 + j, (t % 2) * D:(t % 2 + 1) * D],
                                           acc[:, t, :], ALU.add)
                last.then_inc(bias_ok, 1)
            dve.wait_ge(bias_ok, 4)

            def expert(e, before):
                for m in range(KD):
                    g_low(e, 0, m)
                combine(before, 1)
                for m in range(KD):
                    g_low(e, 1, m)

            with dve.Fori(1, E // 2 - 1) as pair:
                for slot in range(2):
                    expert(pair * 2 + slot, pair * 2 + (slot - 1))
                    combine(pair * 2 + slot, 0)
            expert(E - 2, E - 3)
            combine(E - 2, 0)
            expert(E - 1, E - 2)

            def last_stats(j):
                if j == 1:
                    dve.wait_ge(last_sum, 2)
                else:
                    dve.wait_ge(y_ok, 4 * (E - 1) + max(j, 1))
                for t in (2 * j, 2 * j + 1):
                    v.bn_stats(stats[:, t, :], acc[:, t, :]).then_inc(stats2_ok, 1)
                for t in (2 * j, 2 * j + 1):
                    dve.wait_ge(stats2_ok, t + 1)
                    v.bn_aggr(mv[:, t, :], stats[:, t, :]).then_inc(mv2_ok, 1)

            combine_pair(E - 1, 0)
            last_stats(0)
            combine_pair(E - 1, 2)
            norm_scales(0, sd2_ok, rstd2_ok, shift2_ok)
            last_stats(1)
            combine_pair(E - 1, 3)
            last_stats(2)
            norm_scales(1, sd2_ok, rstd2_ok, shift2_ok)
            last_stats(3)
            norm_scales(2, sd2_ok, rstd2_ok, shift2_ok)
            dve.wait_ge(sd2_ok, 4)
            v.reciprocal(rstd[:, 6:8], sd[:, 6:8]).then_inc(rstd2_ok, 1)
            dve.wait_ge(rstd2_ok, 4)
            for t in (6, 7):
                v.tensor_scalar(z[:, t, :], acc[:, t, :], mv[:, t, 0:1], rstd[:, t:t + 1],
                                ALU.subtract, ALU.mult).then_inc(out_dve_ok, 1)

        @block.tensor
        def _(pe):
            def product(dst, terms):
                for k, (lh, ll, rh, rl) in enumerate(terms):
                    nc.tensor.matmul(dst, lh, rh, start=k == 0, stop=False)
                    nc.tensor.matmul(dst, lh, rl, start=False, stop=False)
                    last = nc.tensor.matmul(dst, ll, rh, start=False, stop=k == len(terms) - 1)
                return last

            def stay_warm(n):
                for _ in range(n):
                    nc.tensor.matmul(ps[:, 1, 0:P], ident[:], ident[:], start=True, stop=True)

            pe.wait_ge(ident_ok, 1)
            stay_warm(WARM_LOADS)
            for t in range(T):
                pe.wait_ge(xT_lo_ok, t // 2 + 1)
                if t >= 4:
                    pe.wait_ge(kv_ok, t - 3)
                for k in range(KD):
                    if t == 0:
                        pe.wait_ge(wkv_lo_ok, k + 1)
                    f_hi, f_lo = fT_hi[:, k, tile(t)], fT_lo[:, k, tile(t)]
                    nc.tensor.matmul(ps[:, t % 4, :], f_hi, wkv_hi[:, k, :], start=k == 0, stop=False)
                    nc.tensor.matmul(ps[:, t % 4, :], f_hi, wkv_lo[:, k, :], start=False, stop=False)
                    last = nc.tensor.matmul(ps[:, t % 4, :], f_lo, wkv_hi[:, k, :], start=False, stop=k == KD - 1)
                last.then_inc(kv_mm, 1)

            def q_half(n):
                for m, bank in zip((0, 2, 1), ((4, 5, 6), (7, 0, 1))[n]):
                    if bank < 4:
                        pe.wait_ge(kv_ok, 4 + bank + 1)
                    product(ps[:, bank, :], [(wq_hi[:, k, tile(m)], wq_lo[:, k, tile(m)],
                                              fT_hi[:, k, half(n)], fT_lo[:, k, half(n)]) for k in range(KD)])\
                        .then_inc(q_mm, 1)

            pe.wait_ge(wq_lo_ok, 1)
            q_half(0)
            pe.wait_ge(kv_ok, T)
            for t in range(T):
                pe.wait_ge(kv_prod, t + 1)
                pe.wait_ge(krec_ok, t // TPH + 1)
                for k in range(KD):
                    last = nc.tensor.matmul(ps[:, 2 + k, 0:1], z[:, t, tile(k)], krec[:, t:t + 1],
                                            start=t == 0, stop=t == T - 1)
            last.then_inc(a_mm, 1)
            q_half(1)

            pe.wait_ge(wo_lo_ok, KD)
            for t in range(T):
                pe.wait_ge(q_rot_lo_ok, t // TPH + 1)
                pe.wait_ge(q_pass_lo_ok, t // TPH + 1)
                if t == 3:
                    pe.wait_ge(qab_ok, 3)
                if t >= 4:
                    pe.wait_ge(z_ok, t - 3)
                product(ps[:, 4 + t % 4, 0:D], [(gT_hi[:, k, tile(t)], gT_lo[:, k, tile(t)],
                                                 wo_hi[:, k, :], wo_lo[:, k, :]) for k in range(KD)])\
                    .then_inc(o_mm, 1)

            def x1_transpose(t):
                pe.wait_ge(x1_ok, t + 1)
                if t == 3:
                    pe.wait_ge(x1_lo_ok, 1)
                if t >= 4:
                    pe.wait_ge(z_ok, t + 1)
                for k in range(KD):
                    last = nc.tensor.transpose(ps[:, X1T_BANK[t], tile(k)], x1[:, t, tile(k)], ident[:])
                last.then_inc(x1T_mm, 1)

            def fc1(e, slot, n):
                for m in range(KD):
                    if not isinstance(e, int) or e > 0:
                        pe.wait_ge(h_ok, e * 4 + (2 * n + m - 3))
                    product(ps[:, 2 * n + m, :],
                            [(w_hi[:, slot, k * D + m * P:k * D + (m + 1) * P],
                              w_lo[:, slot, k * D + m * P:k * D + (m + 1) * P],
                              fT_hi[:, k, half(n)], fT_lo[:, k, half(n)]) for k in range(KD)])\
                        .then_inc(fc1_mm[n], 1)

            def fc2(e, slot, n):
                pe.wait_ge(g_lo_ok, e * 4 + (2 * n + 2))
                for j in (2 * n, 2 * n + 1):
                    if not isinstance(e, int) or e > 0:
                        pe.wait_ge(y_ok, e * 4 + (j - 3))
                    for t in (2 * j, 2 * j + 1):
                        last = product(ps[:, 4 + j, (t % 2) * D:(t % 2 + 1) * D],
                                       [(gT_hi[:, k, tile(t)], gT_lo[:, k, tile(t)],
                                         w_hi[:, slot, (2 + k) * D:(3 + k) * D],
                                         w_lo[:, slot, (2 + k) * D:(3 + k) * D]) for k in range(KD)])
                    last.then_inc(y_mm, 1)

            for j in range(2):
                x1_transpose(2 * j)
                x1_transpose(2 * j + 1)
                stay_warm(WARM_NORM)
            pe.wait_ge(w1_ok, 1)
            pe.wait_ge(x1_lo_ok, 4)
            fc1(0, 0, 0)
            for t in range(4, T):
                x1_transpose(t)
            pe.wait_ge(gate_ok, 1)
            pe.wait_ge(x1_lo_ok, T)
            for n in range(NH):
                for k in range(KD):
                    nc.tensor.matmul(ps[:, 4 + n, :], gpad[:, k, :], fT_hi[:, k, half(n)], start=k == 0, stop=False)
                    last = nc.tensor.matmul(ps[:, 4 + n, :], gpad[:, k, :], fT_lo[:, k, half(n)],
                                            start=False, stop=k == KD - 1)
                last.then_inc(lg_mm, 1)
            fc1(0, 0, 1)
            pe.wait_ge(lgT_ok, 2)
            for t in range(T):
                last = nc.tensor.transpose(ps[:, 6, t * 2 * E:(t + 1) * 2 * E], lgT[:, tile(t)],
                                           ident[0:2 * E, 0:2 * E])
            last.then_inc(lgp_mm, 1)
            pe.wait_ge(w2_ok, 1)
            fc2(0, 0, 0)
            pe.wait_ge(w1_ok, 2)
            fc1(1, 1, 0)
            pe.wait_ge(lgp_ok, 1)
            fc2(0, 0, 1)
            fc1(1, 1, 1)
            pe.wait_ge(comb_p_ok, 1)
            pe.wait_ge(y_ok, 4)
            for t in range(T):
                last = nc.tensor.transpose(ps[0:2 * E, 6 + t // 4, tile(t % 4)], comb_p[:, t, :], ident[:])
                if t % 4 == 3:
                    last.then_inc(combT_mm, 1)
            pe.wait_ge(w2_ok, 2)
            fc2(1, 1, 0)
            pe.wait_ge(combT_ok, 2)
            pe.wait_ge(b2_ok, 1)
            for j in (2, 3, 0, 1):
                if j < 2:
                    pe.wait_ge(y_ok, 4 + j + 1)
                for t in (2 * j, 2 * j + 1):
                    dst = ps[:, 4 + j, (t % 2) * D:(t % 2 + 1) * D]
                    nc.tensor.matmul(dst, combT[:, tile(t)], b2_hi[:], start=True, stop=False)
                    last = nc.tensor.matmul(dst, combT[:, tile(t)], b2_lo[:], start=False, stop=True)
                last.then_inc(bias_mm, 1)
            with pe.Fori(1, E // 2) as pair:
                e0 = pair * 2
                for slot in range(2):
                    pe.wait_ge(w1_ok, e0 + (slot + 1))
                    fc1(e0 + slot, slot, 0)
                    pe.wait_ge(bias_ok, 4)
                    fc2(e0 + (slot - 1), 1 - slot, 1)
                    fc1(e0 + slot, slot, 1)
                    pe.wait_ge(w2_ok, e0 + (slot + 1))
                    fc2(e0 + slot, slot, 0)
            fc2(E - 1, 1, 1)


def kernel(**inputs):
    import concourse.bacc as bacc
    from concourse.bass_utils import run_bass_kernel_spmd

    a = {k.replace("L0_", ""): np.asarray(v) for k, v in inputs.items()}
    x = a["attn_X"][0]
    S, D = x.shape
    T, KD, ROT = S // P, D // P, D // 2

    def blocks(m):
        return m.reshape(-1, P, m.shape[-1]).transpose(1, 0, 2)

    w_in, b_in = a["attn_W_in"], a["attn_b_in"]
    swap = np.arange(ROT) ^ 1
    w_q = np.concatenate([w_in[:D], w_in[:ROT][swap]])
    b_q = np.concatenate([b_in[:D], b_in[:ROT][swap]]).reshape(-1, P).T

    inv_freq = (np.float32(1.0) / np.float32(ROPE_THETA) ** (np.arange(0, ROT, 2, dtype=np.float32)
                                                             / np.float32(ROT))).astype(np.float32)
    angle = np.arange(S, dtype=np.float32)[:, None] * inv_freq[None, :]
    cos, sin = np.cos(angle), np.sin(angle)
    rope_tok = np.stack([t.reshape(T, P, ROT // 2).transpose(1, 0, 2) for t in (cos, sin)], axis=1)
    sign = np.where(np.arange(ROT) % 2 == 0, -1.0, 1.0).astype(np.float32)
    rope_t = np.stack([np.repeat(cos, 2, axis=1).T, np.repeat(sin, 2, axis=1).T * sign[:, None]], axis=1)

    E = a["ffn_gate_w"].shape[1]
    experts = np.concatenate([a["ffn_fc1_w"].reshape(E, KD, P, D), a["ffn_fc2_w"].reshape(E, KD, P, D)],
                             axis=1).transpose(0, 2, 1, 3).reshape(E, P, 4 * D)
    columns = np.concatenate([
        b_q,
        blocks(a["ffn_gate_w"]).reshape(P, -1),
        a["ffn_fc1_b"].reshape(E, KD, P).transpose(2, 0, 1).reshape(P, -1),
        np.broadcast_to(a["ffn_alpha"], (P, E)),
        np.broadcast_to(np.arange(E, 0, -1, dtype=np.float32), (P, E)),
    ], axis=1)
    arrays = {
        "x_tok": x.reshape(T, P, D).transpose(1, 0, 2),
        "x_t": blocks(x.T),
        "w_kv_t": blocks(w_in[D:].T),
        "w_q_t": blocks(w_q.T),
        "w_out_t": blocks(a["attn_W_out"].T),
        "b_rows": np.concatenate([b_in[D:], a["attn_b_out"]]),
        "rope_tok": rope_tok,
        "rope_t": rope_t,
        "columns": columns,
        "expert_w": experts,
        "fc2_b": np.concatenate([a["ffn_fc2_b"]] * 2),
    }
    nc = bacc.Bacc("TRN2", target_bir_lowering=False, num_devices=1)
    send, args = {}, []
    for name, value in arrays.items():
        value = np.ascontiguousarray(value)
        send[f"in_{name}"] = value
        args.append(nc.dram_tensor(f"in_{name}", value.shape, F32, kind="ExternalInput").ap())
    out = nc.dram_tensor("out", (S, D), F32, kind="ExternalOutput")
    layer_kernel(nc, *args, out.ap())
    result = run_bass_kernel_spmd(nc, [send], core_ids=[0])
    return result.results[0]["out"].reshape(1, S, D)
```

```python
from contextlib import ExitStack

import numpy as np

import concourse.bass as bass
from concourse import mybir

ALU = mybir.AluOpType
ACT = mybir.ActivationFunctionType
AX_X = mybir.AxisListType.X
F32 = mybir.dt.float32
F32R = mybir.dt.float32r

P = 128
ROPE_THETA = 10000.0
LN_EPS = 1e-5
NORM_FLOOR = 1e-12
BIAS_LOW = 32
MASKED = -3.0e38
WARM_LOADS = 8
WARM_NORM = 5


def layer_kernel(nc, x_tok, x_t, w_kv_t, w_q_t, w_out_t, b_rows, rope_tok, rope_t,
                 columns, expert_w, fc2_b, out):
    _, T, D = x_tok.shape
    S = T * P
    KD = D // P
    E = expert_w.shape[0]
    ROT = 2 * rope_tok.shape[-1]
    HALF = rope_tok.shape[-1]
    NH = S // 512
    TPH = T // NH
    BIAS_ROWS = BIAS_LOW + 2 * E
    assert (D, KD, NH, E, T) == (256, 2, 2, 8, 8)

    with ExitStack() as ctx:
        def sb(name, shape, dt=F32):
            return ctx.enter_context(nc.sbuf_tensor(name, shape, dt))

        def sem(name):
            return ctx.enter_context(nc.semaphore(name))

        ps = ctx.enter_context(nc.psum_tensor("ps", [P, 8, 512], F32))

        xT = sb("xT", [P, KD, S])
        wkv = sb("wkv", [P, KD, 2 * D])
        wq = sb("wq", [P, KD, D])
        wout = sb("wout", [P, KD, D])
        brow = sb("brow", [P, 3 * D])
        bkv, bout = brow[:, 0:2 * D], brow[:, 2 * D:3 * D]
        rtok = sb("rtok", [P, 2, T, HALF])
        rT = sb("rT", [P, 2, S])
        wraw = sb("wraw", [P, 2, 4 * D])
        cols = sb("cols", [P, columns.shape[1]])
        bq = cols[:, 0:KD]
        gw = cols[:, KD:KD + KD * E].rearrange("p (k e) -> p k e", k=KD)
        b1 = cols[:, KD + KD * E:KD + 2 * KD * E].rearrange("p (e k) -> p e k", k=KD)
        alp = cols[:, KD + 2 * KD * E:KD + 2 * KD * E + E]
        order = cols[:, KD + 2 * KD * E + E:KD + 2 * KD * E + 2 * E]
        b1_now = sb("b1_now", [P, 2, KD])
        b2 = sb("b2", [BIAS_ROWS, D])

        fT_hi = sb("fT_hi", [P, KD, S], F32R)
        fT_lo = sb("fT_lo", [P, KD, S], F32R)
        wkv_hi = sb("wkv_hi", [P, KD, 2 * D], F32R)
        wkv_lo = sb("wkv_lo", [P, KD, 2 * D], F32R)
        wq_hi = sb("wq_hi", [P, KD, D], F32R)
        wq_lo = sb("wq_lo", [P, KD, D], F32R)
        kv = sb("kv", [P, T, 2 * D])
        ksq = sb("ksq", [P, T])
        knorm = sb("knorm", [P, T])
        kfloor = sb("kfloor", [P, T])
        krec = sb("krec", [P, T])
        acol = sb("acol", [P, KD])
        wo_hi = sb("wo_hi", [P, KD, D], F32R)
        wo_lo = sb("wo_lo", [P, KD, D], F32R)
        qa = sb("qa", [P, NH, 512])
        qb = sb("qb", [P, NH, 512])
        qT = sb("qT", [P, KD, S])
        gT_hi = sb("gT_hi", [P, KD, S], F32R)
        gT_lo = sb("gT_lo", [P, KD, S], F32R)

        z = sb("z", [P, T, D])
        acc = sb("acc", [P, T, D])
        x1 = sb("x1", [P, T, D])
        rot_a, rot_b = (x1[:, i * T // 2:(i + 1) * T // 2, :].rearrange("p t (u r) -> p (t u) r", r=ROT)
                        for i in range(2))
        stats = sb("stats", [P, T, 6])
        mv = sb("mv", [P, T, 2])
        sd = sb("sd", [P, T])
        table_unused = sb("table_unused", [P, 2])
        rstd = sb("rstd", [P, T])
        shift = sb("shift", [P, T])
        ident = sb("ident", [P, P])
        eps = sb("eps", [P, 1])
        zero = sb("zero", [P, 1])

        gpad = sb("gpad", [P, KD, P], F32R)
        lgT = sb("lgT", [2 * E, S])
        lgp = sb("lgp", [P, T, 2 * E])
        lg = sb("lg", [P, T, E])
        lg2 = sb("lg2", [P, T, E])
        hit = sb("hit", [P, T, E])
        sel = sb("sel", [P, 2, T, E])
        top = sb("top", [P, 2, T])
        which = sb("which", [P, 2, T])
        gap = sb("gap", [P, T])
        th = sb("th", [P, T])
        wt = sb("wt", [P, 2, T])
        comb = sb("comb", [P, T, E])
        comb_p = sb("comb_p", [P, T, 2 * BIAS_LOW])
        combT = sb("combT", [BIAS_ROWS, S], F32R)
        b2_parts = sb("b2_parts", [BIAS_ROWS, D], F32R)

        w_hi = sb("w_hi", [P, 2, 4 * D], F32R)
        w_lo = sb("w_lo", [P, 2, 4 * D], F32R)
        h = kv[:, 0:2 * NH, :]
        gE_hi, gE_lo = wkv_hi, wkv_lo
        scaled = x1[:, T - 2:T, :]

        l_wq, l_wout, l_brow, l_rtok, l_rT, l_cols, l_b2, l_x = (
            sem(f"l_{n}") for n in "wq wout brow rtok rT cols b2 x".split())
        l_wkv = [sem(f"l_wkv{k}") for k in range(KD)]
        l_xT = [sem(f"l_xT{c}") for c in range(4)]
        l_exp = [sem(f"l_exp{slot}") for slot in range(2)]
        stored = sem("stored")
        wkv_hi_ok, wkv_lo_ok, xT_hi_ok, xT_lo_ok, wq_hi_ok, wq_lo_ok = (
            sem(n) for n in "wkv_hi_ok wkv_lo_ok xT_hi_ok xT_lo_ok wq_hi_ok wq_lo_ok".split())
        kv_mm, kv_ok, rot_parts, rot_ok, vrot_parts, vrot_ok, kv_prod, ksq_ok, knorm_ok, kfloor_ok, krec_ok = (
            sem(n) for n in "kv_mm kv_ok rot_parts rot_ok vrot_parts vrot_ok kv_prod ksq_ok knorm_ok kfloor_ok krec_ok".split())
        q_mm, q_raw_ok, qab_ok, q_other_ok, q_rot_ok, q_pass_ok, q_hi_ok, q_rot_lo0_ok, q_rot_lo1_ok, q_pass_lo_ok = (
            sem(n) for n in "q_mm q_raw_ok qab_ok q_other_ok q_rot_ok q_pass_ok q_hi_ok q_rot_lo0_ok q_rot_lo1_ok q_pass_lo_ok".split())
        a_mm, acol_ok, wo_hi_ok, wo_lo_ok = (sem(n) for n in "a_mm acol_ok wo_hi_ok wo_lo_ok".split())
        o_mm, res_dbl, res_ok, z_ok, stats_ok, mv_ok, sd_ok, rstd_ok, shift_ok, x1_ok, x1_last_ok, x1T_mm, x1_hi_ok, x1_lo_ok = (
            sem(n) for n in "o_mm res_dbl res_ok z_ok stats_ok mv_ok sd_ok rstd_ok shift_ok x1_ok x1_last_ok x1T_mm x1_hi_ok x1_lo_ok".split())
        ident0, ident_ok, gpad0, comb_p0, gate_hi_ok, gate_ok, b2_hi_ok, b2_ok = (
            sem(n) for n in "ident0 ident_ok gpad0 comb_p0 gate_hi_ok gate_ok b2_hi_ok b2_ok".split())
        lg_mm, lgT_ok, lgp_mm, lgp_ok, route, gap_ok, th_ok, comb_p_ok, combT_mm, combT_ok, bias_mm, bias_ok = (
            sem(n) for n in "lg_mm lgT_ok lgp_mm lgp_ok route gap_ok th_ok comb_p_ok combT_mm combT_ok bias_mm bias_ok".split())
        const_ok, b1_ok, w_part, w1_ok, w2_ok, h_ok, g_hi_ok, g_lo_ok, y_mm, y_ok = (
            sem(n) for n in "const_ok b1_ok w_part w1_ok w2_ok h_ok g_hi_ok g_lo_ok y_mm y_ok".split())
        fc1_mm = [sem(f"fc1_mm{n}") for n in range(NH)]
        stats2_ok, mv2_ok, sd2_ok, rstd2_ok, shift2_ok, out_ok, out_dve_ok, y_scaled, last_sum = (
            sem(n) for n in "stats2_ok mv2_ok sd2_ok rstd2_ok shift2_ok out_ok out_dve_ok y_scaled last_sum".split())

        def raw(part):
            return part.bitcast(F32)

        def half(n):
            return slice(n * 512, (n + 1) * 512)

        def tile(t):
            return slice(t * P, (t + 1) * P)

        POOL_ROTATES = ((0, 2), (2, 3), (4, 6), (6, 7))
        DVE_ROTATES = (3, 7)

        def pairs(ap):
            return ap.rearrange("p t (c i) -> p t c i", c=2)

        def rotary_product(t0, t1, part, c):
            tiles = slice(t0, t1)
            return (pairs((rot_a, rot_b)[part][:, tiles, :])[:, :, c, :],
                    pairs(kv[:, tiles, 0:ROT])[:, :, c if part == 0 else 1 - c, :], rtok[:, part, tiles, :])

        def rotary_sum(t0, t1, c):
            tiles = slice(t0, t1)
            return (pairs(kv[:, tiles, 0:ROT])[:, :, c, :], pairs(rot_a[:, tiles, :])[:, :, c, :],
                    pairs(rot_b[:, tiles, :])[:, :, c, :])

        def other_product(n, to, fr):
            return qb[to, n, :], qT[fr, 0, half(n)], rT[fr, 1, half(n)]

        EVEN, ODD = slice(0, HALF), slice(HALF, ROT)
        Q_BANK = ((4, 5), (0, 1))
        X1T_BANK = (2, 3, 0, 2, 2, 3, 6, 7)
        BIAS_BANK = (0, 1, 6, 7)

        def g_parts(e, n, m):
            if e is LAST and n == 1:
                return gE_hi[:, m, :], gE_lo[:, m, :]
            return gT_hi[:, m, half(n)], gT_lo[:, m, half(n)]

        LAST = E - 1
        MADE = ((LAST - 1, 0), (LAST - 1, 1), (LAST - 1, 2), (LAST, 0), (LAST, 1), (LAST - 1, 3), (LAST, 2), (LAST, 3))
        TAKEN = tuple(p for p in MADE if p != (LAST - 1, 3))

        def made(e, j):
            return 4 * (E - 2) + MADE.index((e, j)) + 1 if isinstance(e, int) and e >= LAST - 1 else e * 4 + (j + 1)

        def taken(e, j):
            return 4 * (E - 2) + TAKEN.index((e, j)) + 1 if isinstance(e, int) and e >= LAST - 1 else e * 4 + (j + 1)

        block = ctx.enter_context(nc.Block())

        @block.sync
        def _(sp):
            def load_x_t(c):
                part = slice(c * 256, (c + 1) * 256)
                sp.dma_start(xT[:, :, part], x_t[:, :, part]).then_inc(l_xT[c], 16)

            sp.dma_start(wkv[:, 0, :], w_kv_t[:, 0, :]).then_inc(l_wkv[0], 16)
            load_x_t(0)
            sp.dma_start(wkv[:, 1, :], w_kv_t[:, 1, :]).then_inc(l_wkv[1], 16)
            load_x_t(1)
            sp.dma_start(brow[:], b_rows.partition_broadcast(P)).then_inc(l_brow, 16)
            load_x_t(2)
            load_x_t(3)
            sp.dma_start(rtok[:], rope_tok).then_inc(l_rtok, 16)
            sp.dma_start(wq[:], w_q_t).then_inc(l_wq, 16)
            sp.dma_start(acc[:], x_tok).then_inc(l_x, 16)
            sp.dma_start(cols[:], columns).then_inc(l_cols, 16)
            sp.dma_start(rT[:], rope_t).then_inc(l_rT, 16)
            sp.dma_start(wout[:], w_out_t).then_inc(l_wout, 16)
            sp.dma_start(b2[:], fc2_b).then_inc(l_b2, 16)
            for e in range(2):
                sp.dma_start(wraw[:, e, :], expert_w[e]).then_inc(l_exp[e], 16)
            with sp.Fori(1, E // 2) as pair:
                for slot in range(2):
                    sp.wait_ge(w2_ok, pair * 2 + (slot - 1))
                    sp.dma_start(wraw[:, slot, :], expert_w[bass.ds(pair * 2 + slot, 1)].squeeze(0))\
                      .then_inc(l_exp[slot], 16)
            for j in (0, 1, 3, 2):
                if j < T // 2 - 1:
                    sp.wait_ge(out_ok, 2 * j + 2)
                else:
                    sp.wait_ge(out_dve_ok, 2)
                sp.dma_start(out[2 * j * P:(2 * j + 2) * P, :].rearrange("(t p) d -> p t d", p=P),
                             z[:, 2 * j:2 * j + 2, :]).then_inc(stored, 16)
            sp.wait_ge(stored, 16 * (T // 2))

        @block.gpsimd
        def _(pool):
            g = nc.gpsimd
            g.memset(ident[:], 0.0).then_inc(ident0, 1)
            g.memset(zero[:], 0.0).then_inc(const_ok, 1)
            g.memset(eps[:], LN_EPS).then_inc(const_ok, 1)
            g.memset(raw(gpad[:]), 0.0).then_inc(gpad0, 1)
            g.memset(comb_p[:], 0.0).then_inc(comb_p0, 1)
            pool.wait_ge(ident0, 1)
            g.affine_select(out=ident[:], in_=ident[:], compare_op=ALU.not_equal, fill=1.0, base=0,
                            pattern=[[-1, P]], channel_multiplier=1).then_inc(ident_ok, 1)
            pool.wait_ge(l_rtok, 16)
            for i, (t0, t1) in enumerate(POOL_ROTATES):
                pool.wait_ge(kv_ok, t1)
                for c in range(2):
                    g.tensor_tensor(*rotary_product(t0, t1, 0, c), ALU.mult)
                    g.tensor_tensor(*rotary_product(t0, t1, 1, c), ALU.mult).then_inc(rot_parts, 1)
                pool.wait_ge(rot_parts, 2 * i + 2)
                pool.wait_ge(ksq_ok, t1)
                g.tensor_tensor(*rotary_sum(t0, t1, 0), ALU.subtract)
                g.tensor_tensor(*rotary_sum(t0, t1, 1), ALU.add).then_inc(rot_ok, 1)
            def residual(t0, t1):
                pool.wait_ge(res_dbl, t0 // TPH + 1)
                g.tensor_tensor(acc[:, t0:t1, :], acc[:, t0:t1, :],
                                bout.unsqueeze(1).to_broadcast([P, t1 - t0, D]), ALU.add).then_inc(res_ok, 1)

            pool.wait_ge(l_rT, 16)
            pool.wait_ge(rot_ok, len(POOL_ROTATES))
            def other(n):
                pool.wait_ge(q_raw_ok, n + 1)
                g.tensor_tensor(*other_product(n, EVEN, ODD), ALU.mult).then_inc(q_other_ok, 1)
                pool.wait_ge(q_other_ok, n + 1)

            def q_pass_low(n):
                pool.wait_ge(q_hi_ok, (1, 3)[n])
                g.tensor_tensor(gT_lo[:, 1, half(n)], qT[:, 1, half(n)], raw(gT_hi[:, 1, half(n)]),
                                ALU.subtract).then_inc(q_pass_lo_ok, 1)

            other(0)
            q_pass_low(0)
            pool.wait_ge(q_pass_lo_ok, 1)
            other(1)
            pool.wait_ge(l_brow, 16)
            residual(0, TPH)
            q_pass_low(1)
            pool.wait_ge(q_hi_ok, 4)
            g.tensor_tensor(gT_lo[:, 0, half(1)], qT[:, 0, half(1)], raw(gT_hi[:, 0, half(1)]),
                            ALU.subtract).then_inc(q_rot_lo1_ok, 1)
            residual(4, 6)
            residual(6, 8)

            def split(slot, part, n_parts, ok):
                cols = slice(part * 2 * D, (part + 1) * 2 * D)
                src = wraw[:, slot, cols]
                g.tensor_tensor(w_hi[:, slot, cols], src, zero[:].to_broadcast([P, 2 * D]),
                                ALU.add).then_inc(w_part, 1)
                pool.wait_ge(w_part, n_parts)
                g.tensor_tensor(w_lo[:, slot, cols], src, raw(w_hi[:, slot, cols]), ALU.subtract).then_inc(ok, 1)

            pool.wait_ge(const_ok, 1)
            pool.wait_ge(l_exp[0], 16)
            split(0, 0, 1, w1_ok)
            pool.wait_ge(l_cols, 16)
            pool.wait_ge(gpad0, 1)
            g.tensor_copy(gpad[:, :, 0:E], gw).then_inc(gate_hi_ok, 1)
            pool.wait_ge(gate_hi_ok, 1)
            g.tensor_tensor(gpad[:, :, E:2 * E], gw, raw(gpad[:, :, 0:E]), ALU.subtract).then_inc(gate_ok, 1)
            split(0, 1, 2, w2_ok)
            pool.wait_ge(l_exp[1], 16)
            split(1, 0, 3, w1_ok)
            split(1, 1, 4, w2_ok)
            pool.wait_ge(l_b2, 16)
            pool.wait_ge(w2_ok, 2)
            g.tensor_copy(b2_parts[:], b2[:]).then_inc(b2_hi_ok, 1)
            pool.wait_ge(b2_hi_ok, 1)
            low_rows = slice(BIAS_LOW, BIAS_ROWS)
            g.tensor_tensor(b2_parts[low_rows, :], b2[low_rows, :], raw(b2_parts[low_rows, :]),
                            ALU.subtract).then_inc(b2_ok, 1)
            pool.wait_ge(b2_ok, 1)
            with pool.Fori(1, E // 2) as pair:
                e0 = pair * 2
                for slot in range(2):
                    pool.wait_ge(l_exp[slot], pair * 16 + 16)
                    pool.wait_ge(fc1_mm[1], e0 * 2 + (2 * slot - 2))
                    split(slot, 0, e0 * 2 + (2 * slot + 1), w1_ok)
                    pool.wait_ge(y_mm, e0 * 4 + (4 * slot - 4))
                    split(slot, 1, e0 * 2 + (2 * slot + 2), w2_ok)

            pool.wait_ge(y_ok, taken(LAST - 2, 3))
            for i in range(2):
                pool.wait_ge(y_scaled, i + 1)
                g.tensor_tensor(acc[:, T - 2 + i, :], acc[:, T - 2 + i, :], scaled[:, i, :],
                                ALU.add).then_inc(last_sum, 1)
            pool.wait_ge(y_scaled, 3)
            pool.wait_ge(last_sum, 2)
            g.tensor_tensor(acc[:, T - 1, :], acc[:, T - 1, :], scaled[:, 1, :], ALU.add).then_inc(last_sum, 1)

        @block.scalar
        def _(act):
            a = nc.scalar
            def x_high(c):
                part = slice(c * 256, (c + 1) * 256)
                act.wait_ge(l_xT[c], 16)
                a.copy(fT_hi[:, :, part], xT[:, :, part]).then_inc(xT_hi_ok, 1)

            for k in range(KD):
                act.wait_ge(l_wkv[k], 16)
                a.copy(wkv_hi[:, k, :], wkv[:, k, :]).then_inc(wkv_hi_ok, 1)
                x_high(k)
            x_high(2)
            x_high(3)
            act.wait_ge(l_wq, 16)
            a.copy(wq_hi[:], wq[:]).then_inc(wq_hi_ok, 1)
            for t in range(T):
                act.wait_ge(kv_ok, t + 1)
                a.activation(gT_lo[:, t // TPH, (t % TPH) * D:(t % TPH + 1) * D], kv[:, t, 0:D], ACT.Square,
                             accum_out=ksq[:, t:t + 1]).then_inc(ksq_ok, 1)
                if t % TPH == TPH - 1:
                    act.wait_ge(ksq_ok, t + 1)
                    q4 = slice(t - TPH + 1, t + 1)
                    a.activation(knorm[:, q4], ksq[:, q4], ACT.Sqrt).then_inc(knorm_ok, 1)
                if t in (3, 5):
                    if t == 3:
                        act.wait_ge(l_x, 16)
                    four = slice((t - 3) // 2 * TPH, ((t - 3) // 2 + 1) * TPH)
                    a.mul(acc[:, four, :], acc[:, four, :], 2.0).then_inc(res_dbl, 1)
            act.wait_ge(l_cols, 16)

            def q_raw(n):
                act.wait_ge(q_mm, 2 * n + 1)
                a.activation(qT[:, 0, half(n)], ps[:, Q_BANK[n][0], :], ACT.Identity,
                             bias=bq[:, 0:1]).then_inc(q_raw_ok, 1)

            def q_pass(n):
                act.wait_ge(q_mm, 2 * n + 2)
                a.activation(qT[:, 1, half(n)], ps[:, Q_BANK[n][1], :], ACT.Identity,
                             bias=bq[:, 1:2]).then_inc(q_pass_ok, 1)
                act.wait_ge(q_pass_ok, n + 1)
                a.copy(gT_hi[:, 1, half(n)], qT[:, 1, half(n)]).then_inc(q_hi_ok, 1)

            def q_rot_high(n):
                act.wait_ge(q_rot_ok, n + 1)
                a.copy(gT_hi[:, 0, half(n)], qT[:, 0, half(n)]).then_inc(q_hi_ok, 1)

            q_raw(0)
            q_pass(0)
            q_raw(1)
            q_rot_high(0)
            act.wait_ge(l_wout, 16)
            act.wait_ge(acol_ok, 1)
            for k in range(KD):
                a.activation(wo_hi[:, k, :], wout[:, k, :], ACT.Copy, scale=acol[:, k:k + 1]).then_inc(wo_hi_ok, 1)
            q_pass(1)
            q_rot_high(1)

            def root(j):
                act.wait_ge(mv_ok, 2 * j + 2)
                a.activation(sd[:, 2 * j:2 * j + 2], mv[:, 2 * j:2 * j + 2, 1], ACT.Sqrt,
                             bias=eps[:]).then_inc(sd_ok, 1)

            def x1_high(t):
                act.wait_ge(x1T_mm, t + 1)
                a.copy(fT_hi[:, :, tile(t)], ps[:, X1T_BANK[t], 0:D].rearrange("p (k c) -> p k c", k=KD))\
                 .then_inc(x1_hi_ok, 1)

            act.wait_ge(const_ok, 2)
            def normalise(j, src, dst, shifts, done):
                act.wait_ge(shifts, j + 1)
                for t in (2 * j, 2 * j + 1):
                    a.activation(dst[:, t, :], src[:, t, :], ACT.Identity, scale=rstd[:, t:t + 1],
                                 bias=shift[:, t:t + 1]).then_inc(done, 1)

            root(0)
            normalise(0, z, x1, shift_ok, x1_ok)
            root(1)
            x1_high(0)
            x1_high(1)
            normalise(1, z, x1, shift_ok, x1_ok)
            root(2)
            x1_high(2)
            x1_high(3)
            normalise(2, z, x1, shift_ok, x1_ok)
            root(3)
            a.activation(table_unused[:, 0:1], eps[:], ACT.Gelu)
            def gelu(e, n, m, bias):
                i = 2 * n + m
                act.wait_ge(fc1_mm[n], e * 2 + (m + 1))
                if not isinstance(e, int) or e > 0:
                    act.wait_ge(g_lo_ok, e * 4 + (i - 3))
                a.activation(h[:, i, :], ps[:, i, :], ACT.Gelu, bias=bias[:, m:m + 1]).then_inc(h_ok, 1)
                act.wait_ge(h_ok, e * 4 + (i + 1))
                a.copy(g_parts(e, n, m)[0], h[:, i, :]).then_inc(g_hi_ok, 1)

            for t in range(4, T):
                x1_high(t)
            gelu(0, 0, 0, b1[:, 0, :])
            gelu(0, 0, 1, b1[:, 0, :])
            for n in range(NH):
                act.wait_ge(lg_mm, n + 1)
                a.copy(lgT[:, half(n)], ps[0:2 * E, 4 + n, :]).then_inc(lgT_ok, 1)
            gelu(0, 1, 0, b1[:, 0, :])
            act.wait_ge(lgp_mm, 1)
            a.copy(lgp[:], ps[:, 6, 0:T * 2 * E].rearrange("p (t c) -> p t c", t=T)).then_inc(lgp_ok, 1)
            gelu(0, 1, 1, b1[:, 0, :])
            act.wait_ge(gap_ok, 1)
            a.activation(th[:], gap[:], ACT.Tanh, scale=0.5).then_inc(th_ok, 1)
            for n in range(NH):
                for m in range(KD):
                    gelu(1, n, m, b1[:, 1, :])
            for c in range(2):
                act.wait_ge(combT_mm, c + 1)
                a.copy(combT[:, half(c)], ps[0:BIAS_ROWS, 6 + c, :]).then_inc(combT_ok, 1)
            with act.Fori(1, E // 2 - 1) as pair:
                e0 = pair * 2
                a.copy(b1_now[:], b1[:, bass.ds(e0, 2), :]).then_inc(b1_ok, 1)
                act.wait_ge(b1_ok, pair)
                for slot in range(2):
                    for n in range(NH):
                        for m in range(KD):
                            gelu(e0 + slot, n, m, b1_now[:, slot, :])
            for e in (LAST - 1, LAST):
                for n in range(NH):
                    for m in range(KD):
                        gelu(e, n, m, b1[:, e, :])
            a.activation(table_unused[:, 1:2], eps[:], ACT.Sqrt)
            act.wait_ge(y_mm, made(LAST - 1, 3))
            for i in range(2):
                a.activation(scaled[:, i, :], ps[:, 7, i * D:(i + 1) * D], ACT.Copy,
                             scale=comb[:, T - 2 + i, LAST - 1:LAST]).then_inc(y_scaled, 1)

            def root2(j):
                act.wait_ge(mv2_ok, 2 * j + 2)
                a.activation(sd[:, 2 * j:2 * j + 2], mv[:, 2 * j:2 * j + 2, 1], ACT.Sqrt,
                             bias=eps[:]).then_inc(sd2_ok, 1)

            root2(0)
            root2(1)
            normalise(0, acc, z, shift2_ok, out_ok)
            act.wait_ge(y_mm, made(LAST, 3))
            act.wait_ge(last_sum, 2)
            a.activation(scaled[:, 1, :], ps[:, 7, D:2 * D], ACT.Copy,
                         scale=comb[:, T - 1, LAST:E]).then_inc(y_scaled, 1)
            normalise(1, acc, z, shift2_ok, out_ok)
            root2(2)
            root2(3)
            normalise(2, acc, z, shift2_ok, out_ok)

        @block.vector
        def _(dve):
            v = nc.vector

            def kv_low(k):
                dve.wait_ge(wkv_hi_ok, k + 1)
                v.tensor_tensor(wkv_lo[:, k, :], wkv[:, k, :], raw(wkv_hi[:, k, :]),
                                ALU.subtract).then_inc(wkv_lo_ok, 1)

            def x_low(c):
                part = slice(c * 256, (c + 1) * 256)
                dve.wait_ge(xT_hi_ok, c + 1)
                v.tensor_tensor(fT_lo[:, :, part], xT[:, :, part], raw(fT_hi[:, :, part]),
                                ALU.subtract).then_inc(xT_lo_ok, 1)

            def kv_out(t):
                dve.wait_ge(kv_mm, t + 1)
                v.tensor_tensor(kv[:, t, :], ps[:, t % 4, :], bkv, ALU.add).then_inc(kv_ok, 1)

            def rotate(t):
                i = DVE_ROTATES.index(t)
                dve.wait_ge(kv_ok, t + 1)
                for c in range(2):
                    v.tensor_tensor(*rotary_product(t, t + 1, 0, c), ALU.mult)
                    v.tensor_tensor(*rotary_product(t, t + 1, 1, c), ALU.mult).then_inc(vrot_parts, 1)
                dve.wait_ge(vrot_parts, 2 * i + 2)
                dve.wait_ge(ksq_ok, t + 1)
                v.tensor_tensor(*rotary_sum(t, t + 1, 0), ALU.subtract)
                v.tensor_tensor(*rotary_sum(t, t + 1, 1), ALU.add).then_inc(vrot_ok, 1)

            def kv_product(t):
                if t in DVE_ROTATES:
                    dve.wait_ge(vrot_ok, DVE_ROTATES.index(t) + 1)
                else:
                    dve.wait_ge(rot_ok, [t < t1 for _, t1 in POOL_ROTATES].index(True) + 1)
                v.tensor_tensor(z[:, t, :], kv[:, t, 0:D], kv[:, t, D:2 * D], ALU.mult).then_inc(kv_prod, 1)

            def k_reciprocal(n):
                q4 = slice(n * TPH, (n + 1) * TPH)
                dve.wait_ge(knorm_ok, n + 1)
                v.tensor_scalar(kfloor[:, q4], knorm[:, q4], NORM_FLOOR, None, ALU.max).then_inc(kfloor_ok, 1)
                dve.wait_ge(kfloor_ok, n + 1)
                v.reciprocal(krec[:, q4], kfloor[:, q4]).then_inc(krec_ok, 1)

            kv_low(0)
            x_low(0)
            kv_low(1)
            x_low(1)
            dve.wait_ge(l_brow, 16)
            kv_out(0)
            x_low(2)
            kv_out(1)
            x_low(3)
            kv_out(2)
            kv_out(3)
            dve.wait_ge(l_rtok, 16)
            rotate(3)
            kv_out(4)
            dve.wait_ge(wq_hi_ok, 1)
            v.tensor_tensor(wq_lo[:], wq[:], raw(wq_hi[:]), ALU.subtract).then_inc(wq_lo_ok, 1)
            kv_product(0)
            kv_out(5)
            kv_product(1)
            kv_product(2)
            kv_out(6)
            kv_product(3)
            k_reciprocal(0)
            kv_out(7)
            rotate(7)
            k_reciprocal(1)
            for t in range(4, T):
                kv_product(t)

            def q_products(n):
                dve.wait_ge(q_raw_ok, n + 1)
                v.tensor_tensor(qa[:, n, :], qT[:, 0, half(n)], rT[:, 0, half(n)], ALU.mult).then_inc(qab_ok, 1)
                if n == 1:
                    dve.wait_ge(q_hi_ok, 2)
                    v.tensor_tensor(gT_lo[:, 0, half(0)], qT[:, 0, half(0)], raw(gT_hi[:, 0, half(0)]),
                                    ALU.subtract).then_inc(q_rot_lo0_ok, 1)
                    dve.wait_ge(a_mm, 1)
                    v.tensor_copy(acol[:], ps[:, 2:4, 0]).then_inc(acol_ok, 1)
                v.tensor_tensor(*other_product(n, ODD, EVEN), ALU.mult).then_inc(qab_ok, 1)

            def q_rotate(n):
                dve.wait_ge(qab_ok, 2 * n + 2)
                dve.wait_ge(q_other_ok, n + 1)
                v.tensor_tensor(qT[:, 0, half(n)], qa[:, n, :], qb[:, n, :], ALU.add).then_inc(q_rot_ok, 1)

            dve.wait_ge(l_rT, 16)
            q_products(0)
            q_rotate(0)
            q_products(1)
            for k in range(KD):
                dve.wait_ge(wo_hi_ok, k + 1)
                v.scalar_tensor_tensor(out=wo_lo[:, k, :], in0=wout[:, k, :], scalar=acol[:, k:k + 1],
                                       in1=raw(wo_hi[:, k, :]), op0=ALU.mult,
                                       op1=ALU.subtract).then_inc(wo_lo_ok, 1)
            q_rotate(1)

            def first_sum(j):
                for t in (2 * j, 2 * j + 1):
                    dve.wait_ge(o_mm, t + 1)
                    v.tensor_tensor(z[:, t, :], ps[:, 4 + t % 4, 0:D], acc[:, t, :], ALU.add).then_inc(z_ok, 1)

            def first_stats(j):
                for t in (2 * j, 2 * j + 1):
                    dve.wait_ge(z_ok, t + 1)
                    v.bn_stats(stats[:, t, :], z[:, t, :]).then_inc(stats_ok, 1)
                for t in (2 * j, 2 * j + 1):
                    dve.wait_ge(stats_ok, t + 1)
                    v.bn_aggr(mv[:, t, :], stats[:, t, :]).then_inc(mv_ok, 1)

            def norm_scales(j, roots, recs, done):
                two = slice(2 * j, 2 * j + 2)
                dve.wait_ge(roots, j + 1)
                v.reciprocal(rstd[:, two], sd[:, two]).then_inc(recs, 1)
                dve.wait_ge(recs, j + 1)
                v.scalar_tensor_tensor(out=shift[:, two], in0=mv[:, two, 0], scalar=-1.0, in1=rstd[:, two],
                                       op0=ALU.mult, op1=ALU.mult).then_inc(done, 1)

            def x1_low(t):
                dve.wait_ge(x1_hi_ok, t + 1)
                v.tensor_tensor(fT_lo[:, :, tile(t)], ps[:, X1T_BANK[t], 0:D].rearrange("p (k c) -> p k c", k=KD),
                                raw(fT_hi[:, :, tile(t)]), ALU.subtract).then_inc(x1_lo_ok, 1)

            dve.wait_ge(res_ok, 1)
            first_sum(0)
            first_stats(0)
            first_sum(1)
            norm_scales(0, sd_ok, rstd_ok, shift_ok)
            first_stats(1)
            dve.wait_ge(res_ok, 2)
            first_sum(2)
            norm_scales(1, sd_ok, rstd_ok, shift_ok)
            x1_low(0)
            x1_low(1)
            first_stats(2)
            dve.wait_ge(res_ok, 3)
            first_sum(3)
            x1_low(2)
            x1_low(3)
            norm_scales(2, sd_ok, rstd_ok, shift_ok)
            first_stats(3)

            def normalise_last(src, dst, roots, recs, done):
                dve.wait_ge(roots, T // 2)
                v.reciprocal(rstd[:, T - 2:T], sd[:, T - 2:T]).then_inc(recs, 1)
                dve.wait_ge(recs, T // 2)
                for t in (T - 2, T - 1):
                    v.tensor_scalar(dst[:, t, :], src[:, t, :], mv[:, t, 0:1], rstd[:, t:t + 1],
                                    ALU.subtract, ALU.mult).then_inc(done, 1)

            normalise_last(z, x1, sd_ok, rstd_ok, x1_last_ok)
            for t in range(4, T):
                x1_low(t)

            def g_low(e, n, m):
                i = 2 * n + m
                dve.wait_ge(g_hi_ok, e * 4 + (i + 1))
                high, low = g_parts(e, n, m)
                v.tensor_tensor(low, h[:, i, :], raw(high), ALU.subtract).then_inc(g_lo_ok, 1)

            def combine_pair(e, j, first=False):
                dve.wait_ge(y_mm, made(e, j))
                if e is LAST and j == 3:
                    dve.wait_ge(last_sum, 2)
                    dve.wait_ge(y_scaled, 3)
                elif not first:
                    dve.wait_ge(y_ok, taken(e - 1, j))
                for t in (2 * j,) if e is LAST and j == 3 else (2 * j, 2 * j + 1):
                    w = comb[:, t, e:e + 1] if isinstance(e, int) else comb[:, t, bass.ds(e, 1)]
                    last = v.scalar_tensor_tensor(
                        out=acc[:, t, :], in0=ps[:, 4 + j, (t % 2) * D:(t % 2 + 1) * D], scalar=w,
                        in1=(x1 if first else acc)[:, t, :], op0=ALU.mult, op1=ALU.add)
                last.then_inc(y_ok, 1)

            def combine(e, n, first=False):
                combine_pair(e, 2 * n, first)
                combine_pair(e, 2 * n + 1, first)

            g_low(0, 0, 0)
            g_low(0, 0, 1)
            g_low(0, 1, 0)

            steps = [0]

            def step(ins):
                steps[0] += 1
                ins.then_inc(route, 1)
                dve.wait_ge(route, steps[0])

            def per_tile(ap):
                return ap.unsqueeze(2).to_broadcast([P, T, E])

            order_b = order.unsqueeze(1).to_broadcast([P, T, E])
            dve.wait_ge(lgp_ok, 1)
            step(v.tensor_tensor(lg[:], lgp[:, :, 0:E], lgp[:, :, E:2 * E], ALU.add))

            def largest(k, src):
                step(v.reduce_max(top[:, k, :], src[:], axis=AX_X))
                step(v.tensor_tensor(hit[:], src[:], per_tile(top[:, k, :]), ALU.is_equal))
                step(v.tensor_tensor(hit[:], hit[:], order_b, ALU.mult))
                step(v.reduce_max(which[:, k, :], hit[:], axis=AX_X))
                step(v.tensor_tensor(sel[:, k, :, :], order_b, per_tile(which[:, k, :]), ALU.is_equal))

            largest(0, lg)
            g_low(0, 1, 1)
            step(v.scalar_tensor_tensor(out=lg2[:], in0=sel[:, 0, :, :], scalar=MASKED, in1=lg[:],
                                        op0=ALU.mult, op1=ALU.add))
            largest(1, lg2)
            v.tensor_tensor(gap[:], top[:, 0, :], top[:, 1, :], ALU.subtract).then_inc(gap_ok, 1)
            dve.wait_ge(th_ok, 1)
            v.tensor_scalar(wt[:, 0, :], th[:], 0.5, 0.5, ALU.mult, ALU.add)
            step(v.tensor_scalar(wt[:, 1, :], th[:], -0.5, 0.5, ALU.mult, ALU.add))
            v.tensor_tensor(hit[:], sel[:, 0, :, :], per_tile(wt[:, 0, :]), ALU.mult)
            step(v.tensor_tensor(lg2[:], sel[:, 1, :, :], per_tile(wt[:, 1, :]), ALU.mult))
            step(v.tensor_tensor(lg[:], hit[:], lg2[:], ALU.add))
            step(v.tensor_tensor(comb[:], lg[:], alp.unsqueeze(1).to_broadcast([P, T, E]), ALU.mult))
            dve.wait_ge(comb_p0, 1)
            copies = comb_p[:].rearrange("p t (i c) -> p t i c", i=2)
            comb_b = comb[:].unsqueeze(2).to_broadcast([P, T, 2, E])
            step(v.tensor_copy(copies[:, :, :, 0:E].bitcast(F32R), comb_b))
            v.tensor_tensor(copies[:, :, :, E:2 * E], comb_b, copies[:, :, :, 0:E], ALU.subtract)\
             .then_inc(comb_p_ok, 1)

            combine(0, 0, first=True)
            combine(0, 1, first=True)
            for m in range(KD):
                g_low(1, 0, m)
            for m in range(KD):
                g_low(1, 1, m)

            for j in range(T // 2):
                dve.wait_ge(bias_mm, j + 1)
                dve.wait_ge(y_ok, j + 1)
                v.tensor_tensor(acc[:, 2 * j:2 * j + 2, :],
                                ps[:, BIAS_BANK[j], :].rearrange("p (t d) -> p t d", t=2),
                                acc[:, 2 * j:2 * j + 2, :], ALU.add).then_inc(bias_ok, 1)
            dve.wait_ge(bias_ok, 4)
            combine(1, 0)

            def expert(e, before):
                for m in range(KD):
                    g_low(e, 0, m)
                combine(before, 1)
                for m in range(KD):
                    g_low(e, 1, m)

            with dve.Fori(1, E // 2 - 1) as pair:
                for slot in range(2):
                    expert(pair * 2 + slot, pair * 2 + (slot - 1))
                    combine(pair * 2 + slot, 0)
            expert(LAST - 1, LAST - 2)
            combine(LAST - 1, 0)

            def last_stats(j):
                dve.wait_ge(y_ok, taken(LAST, j))
                for t in (2 * j, 2 * j + 1):
                    if t == T - 1:
                        dve.wait_ge(last_sum, 3)
                    v.bn_stats(stats[:, t, :], acc[:, t, :]).then_inc(stats2_ok, 1)
                for t in (2 * j, 2 * j + 1):
                    dve.wait_ge(stats2_ok, t + 1)
                    v.bn_aggr(mv[:, t, :], stats[:, t, :]).then_inc(mv2_ok, 1)

            g_low(LAST, 0, 0)
            g_low(LAST, 0, 1)
            g_low(LAST, 1, 0)
            combine_pair(LAST - 1, 2)
            g_low(LAST, 1, 1)
            combine_pair(LAST, 0)
            last_stats(0)
            combine_pair(LAST, 1)
            last_stats(1)
            norm_scales(0, sd2_ok, rstd2_ok, shift2_ok)
            combine_pair(LAST, 2)
            norm_scales(1, sd2_ok, rstd2_ok, shift2_ok)
            last_stats(2)
            combine_pair(LAST, 3)
            last_stats(3)
            norm_scales(2, sd2_ok, rstd2_ok, shift2_ok)
            normalise_last(acc, z, sd2_ok, rstd2_ok, out_dve_ok)

        @block.tensor
        def _(pe):
            def product(dst, terms):
                for k, (lh, ll, rh, rl) in enumerate(terms):
                    nc.tensor.matmul(dst, lh, rh, start=k == 0, stop=False)
                    nc.tensor.matmul(dst, lh, rl, start=False, stop=False)
                    last = nc.tensor.matmul(dst, ll, rh, start=False, stop=k == len(terms) - 1)
                return last

            def stay_warm(n):
                for _ in range(n):
                    nc.tensor.matmul(ps[:, 1, 0:P], ident[:], ident[:], start=True, stop=True)

            pe.wait_ge(ident_ok, 1)
            stay_warm(WARM_LOADS)
            for t in range(T):
                pe.wait_ge(xT_lo_ok, t // 2 + 1)
                if t >= 4:
                    pe.wait_ge(kv_ok, t - 3)
                for k in range(KD):
                    if t == 0:
                        pe.wait_ge(wkv_lo_ok, k + 1)
                    f_hi, f_lo = fT_hi[:, k, tile(t)], fT_lo[:, k, tile(t)]
                    nc.tensor.matmul(ps[:, t % 4, :], f_hi, wkv_hi[:, k, :], start=k == 0, stop=False)
                    nc.tensor.matmul(ps[:, t % 4, :], f_hi, wkv_lo[:, k, :], start=False, stop=False)
                    last = nc.tensor.matmul(ps[:, t % 4, :], f_lo, wkv_hi[:, k, :], start=False, stop=k == KD - 1)
                last.then_inc(kv_mm, 1)

            def q_block(n, m):
                bank = Q_BANK[n][m]
                if bank < 4:
                    pe.wait_ge(kv_ok, 4 + bank + 1)
                product(ps[:, bank, :], [(wq_hi[:, k, tile(m)], wq_lo[:, k, tile(m)],
                                          fT_hi[:, k, half(n)], fT_lo[:, k, half(n)]) for k in range(KD)])\
                    .then_inc(q_mm, 1)

            def feature_sum(n):
                pe.wait_ge(krec_ok, n + 1)
                for t in range(n * TPH, (n + 1) * TPH):
                    pe.wait_ge(kv_prod, t + 1)
                    for k in range(KD):
                        last = nc.tensor.matmul(ps[:, 2 + k, 0:1], z[:, t, tile(k)], krec[:, t:t + 1],
                                                start=t == 0, stop=t == T - 1)
                return last

            pe.wait_ge(wq_lo_ok, 1)
            q_block(0, 0)
            q_block(0, 1)
            pe.wait_ge(kv_ok, T)
            feature_sum(0)
            q_block(1, 0)
            feature_sum(1).then_inc(a_mm, 1)
            q_block(1, 1)

            def x1_transpose(t):
                if t < T - 2:
                    pe.wait_ge(x1_ok, t + 1)
                else:
                    pe.wait_ge(x1_last_ok, t - (T - 3))
                if t == 3:
                    pe.wait_ge(x1_lo_ok, 1)
                if X1T_BANK[t] >= 4:
                    pe.wait_ge(z_ok, t + 1)
                for k in range(KD):
                    last = nc.tensor.transpose(ps[:, X1T_BANK[t], tile(k)], x1[:, t, tile(k)], ident[:])
                last.then_inc(x1T_mm, 1)

            pe.wait_ge(wo_lo_ok, KD)
            for t in range(T):
                pe.wait_ge(q_rot_lo0_ok if t < TPH else q_rot_lo1_ok, 1)
                pe.wait_ge(q_pass_lo_ok, t // TPH + 1)
                if t >= 4:
                    pe.wait_ge(z_ok, t - 3)
                product(ps[:, 4 + t % 4, 0:D], [(gT_hi[:, k, tile(t)], gT_lo[:, k, tile(t)],
                                                 wo_hi[:, k, :], wo_lo[:, k, :]) for k in range(KD)])\
                    .then_inc(o_mm, 1)
                if t == 5:
                    x1_transpose(0)
                    x1_transpose(1)

            def fc1_block(e, slot, n, m):
                if not isinstance(e, int) or e > 0:
                    pe.wait_ge(h_ok, e * 4 + (2 * n + m - 3))
                product(ps[:, 2 * n + m, :],
                        [(w_hi[:, slot, k * D + m * P:k * D + (m + 1) * P],
                          w_lo[:, slot, k * D + m * P:k * D + (m + 1) * P],
                          fT_hi[:, k, half(n)], fT_lo[:, k, half(n)]) for k in range(KD)])\
                    .then_inc(fc1_mm[n], 1)

            def fc1(e, slot, n):
                for m in range(KD):
                    fc1_block(e, slot, n, m)

            def fc2_pair(e, slot, j):
                if e is LAST and j == 3:
                    pe.wait_ge(y_scaled, 2)
                elif not isinstance(e, int) or e > 0:
                    pe.wait_ge(y_ok, taken(e - 1, j))
                g = [g_parts(e, j // 2, k) for k in range(KD)]
                for t in (2 * j, 2 * j + 1):
                    last = product(ps[:, 4 + j, (t % 2) * D:(t % 2 + 1) * D],
                                   [(g[k][0][:, tile(t % TPH)], g[k][1][:, tile(t % TPH)],
                                     w_hi[:, slot, (2 + k) * D:(3 + k) * D],
                                     w_lo[:, slot, (2 + k) * D:(3 + k) * D]) for k in range(KD)])
                last.then_inc(y_mm, 1)

            def fc2(e, slot, n):
                pe.wait_ge(g_lo_ok, e * 4 + (2 * n + 2))
                fc2_pair(e, slot, 2 * n)
                fc2_pair(e, slot, 2 * n + 1)

            x1_transpose(2)
            x1_transpose(3)
            stay_warm(WARM_NORM)
            pe.wait_ge(w1_ok, 1)
            pe.wait_ge(x1_lo_ok, TPH)
            for m in range(KD):
                fc1_block(0, 0, 0, m)
                x1_transpose(4 + 2 * m)
                x1_transpose(5 + 2 * m)
            pe.wait_ge(gate_ok, 1)
            for n in range(NH):
                pe.wait_ge(x1_lo_ok, (n + 1) * TPH)
                for k in range(KD):
                    nc.tensor.matmul(ps[:, 4 + n, :], gpad[:, k, :], fT_hi[:, k, half(n)], start=k == 0, stop=False)
                    last = nc.tensor.matmul(ps[:, 4 + n, :], gpad[:, k, :], fT_lo[:, k, half(n)],
                                            start=False, stop=k == KD - 1)
                last.then_inc(lg_mm, 1)
            fc1(0, 0, 1)
            pe.wait_ge(lgT_ok, 2)
            for t in range(T):
                last = nc.tensor.transpose(ps[:, 6, t * 2 * E:(t + 1) * 2 * E], lgT[:, tile(t)],
                                           ident[0:2 * E, 0:2 * E])
            last.then_inc(lgp_mm, 1)
            pe.wait_ge(w2_ok, 1)
            fc2(0, 0, 0)
            pe.wait_ge(w1_ok, 2)
            fc1(1, 1, 0)
            pe.wait_ge(lgp_ok, 1)
            fc2(0, 0, 1)
            fc1(1, 1, 1)
            pe.wait_ge(comb_p_ok, 1)
            pe.wait_ge(y_ok, 4)
            for t in range(T):
                last = nc.tensor.transpose(ps[0:BIAS_ROWS, 6 + t // 4, tile(t % 4)], comb_p[:, t, 0:BIAS_ROWS],
                                           ident[:])
                if t % 4 == 3:
                    last.then_inc(combT_mm, 1)
            pe.wait_ge(w2_ok, 2)
            pe.wait_ge(g_lo_ok, 6)
            fc2_pair(1, 1, 0)
            pe.wait_ge(b2_ok, 1)
            for j in range(T // 2):
                pe.wait_ge(combT_ok, j // 2 + 1)
                for t in (2 * j, 2 * j + 1):
                    last = nc.tensor.matmul(ps[:, BIAS_BANK[j], (t % 2) * D:(t % 2 + 1) * D], combT[:, tile(t)],
                                            b2_parts[:], start=True, stop=True)
                last.then_inc(bias_mm, 1)
            fc2_pair(1, 1, 1)

            def expert(e, before, slot):
                pe.wait_ge(w1_ok, e + 1)
                pe.wait_ge(bias_ok, 2)
                fc1(e, slot, 0)
                pe.wait_ge(bias_ok, T // 2)
                fc2(before, 1 - slot, 1)
                fc1(e, slot, 1)
                pe.wait_ge(w2_ok, e + 1)
                fc2(e, slot, 0)

            with pe.Fori(1, E // 2 - 1) as pair:
                for slot in range(2):
                    expert(pair * 2 + slot, pair * 2 + (slot - 1), slot)
            expert(LAST - 1, LAST - 2, 0)
            pe.wait_ge(w1_ok, E)
            fc1(LAST, 1, 0)
            fc1(LAST, 1, 1)
            pe.wait_ge(g_lo_ok, 4 * (E - 1))
            fc2_pair(LAST - 1, 0, 2)
            pe.wait_ge(w2_ok, E)
            fc2(LAST, 1, 0)
            fc2_pair(LAST - 1, 0, 3)
            fc2(LAST, 1, 1)


def kernel(**inputs):
    import concourse.bacc as bacc
    from concourse.bass_utils import run_bass_kernel_spmd

    a = {k.replace("L0_", ""): np.asarray(v) for k, v in inputs.items()}
    x = a["attn_X"][0]
    S, D = x.shape
    T, KD, ROT = S // P, D // P, D // 2

    def blocks(m):
        return m.reshape(-1, P, m.shape[-1]).transpose(1, 0, 2)

    order = np.concatenate([np.arange(0, ROT, 2), np.arange(1, ROT, 2), np.arange(ROT, D)])
    w_in = a["attn_W_in"].reshape(3, D, D)[:, order].reshape(3 * D, D)
    b_in = a["attn_b_in"].reshape(3, D)[:, order].reshape(3 * D)
    w_out = a["attn_W_out"][:, order]

    inv_freq = (np.float32(1.0) / np.float32(ROPE_THETA) ** (np.arange(0, ROT, 2, dtype=np.float32)
                                                             / np.float32(ROT))).astype(np.float32)
    angle = np.arange(S, dtype=np.float32)[:, None] * inv_freq[None, :]
    cos, sin = np.cos(angle), np.sin(angle)
    rope_tok = np.stack([t.reshape(T, P, ROT // 2).transpose(1, 0, 2) for t in (cos, sin)], axis=1)
    rope_t = np.stack([np.concatenate([cos.T, cos.T]), np.concatenate([sin.T, -sin.T])], axis=1)

    E = a["ffn_gate_w"].shape[1]
    experts = np.concatenate([a["ffn_fc1_w"].reshape(E, KD, P, D), a["ffn_fc2_w"].reshape(E, KD, P, D)],
                             axis=1).transpose(0, 2, 1, 3).reshape(E, P, 4 * D)
    columns = np.concatenate([
        blocks(b_in[:D, None]).reshape(P, -1),
        blocks(a["ffn_gate_w"]).reshape(P, -1),
        a["ffn_fc1_b"].reshape(E, KD, P).transpose(2, 0, 1).reshape(P, -1),
        np.broadcast_to(a["ffn_alpha"], (P, E)),
        np.broadcast_to(np.arange(E, 0, -1, dtype=np.float32), (P, E)),
    ], axis=1)
    arrays = {
        "x_tok": x.reshape(T, P, D).transpose(1, 0, 2),
        "x_t": blocks(x.T),
        "w_kv_t": blocks(w_in[D:].T),
        "w_q_t": blocks(w_in[:D].T),
        "w_out_t": blocks(w_out.T),
        "b_rows": np.concatenate([b_in[D:], a["attn_b_out"]]),
        "rope_tok": rope_tok,
        "rope_t": rope_t,
        "columns": columns,
        "expert_w": experts,
        "fc2_b": np.concatenate([a["ffn_fc2_b"]] * ((BIAS_LOW + 2 * E) // E)),
    }
    nc = bacc.Bacc("TRN2", target_bir_lowering=False, num_devices=1)
    send, args = {}, []
    for name, value in arrays.items():
        value = np.ascontiguousarray(value)
        send[f"in_{name}"] = value
        args.append(nc.dram_tensor(f"in_{name}", value.shape, F32, kind="ExternalInput").ap())
    out = nc.dram_tensor("out", (S, D), F32, kind="ExternalOutput")
    layer_kernel(nc, *args, out.ap())
    result = run_bass_kernel_spmd(nc, [send], core_ids=[0])
    return result.results[0]["out"].reshape(1, S, D)
```
